# Optimizing a Trainium2 kernel written in Bass

```python
import numpy as np
import jax
import jax.numpy as jnp

def _softmax(x, axis=-1):
    return jax.nn.softmax(x, axis=axis)

def _gelu(x):
    return jax.nn.gelu(x, approximate=True)

def _silu(x):
    return jax.nn.silu(x)

def _sigmoid(x):
    return jax.nn.sigmoid(x)

def _layernorm(x, axis=-1, eps=1e-05):
    m = jnp.mean(x, axis=axis, keepdims=True)
    v = jnp.var(x, axis=axis, keepdims=True)
    return (x - m) / jnp.sqrt(v + eps)

def _scatter_add(tgt, idx, src, axis=0):
    return tgt.at[idx].add(src)

def _segment_sum(src, seg, n):
    return jax.ops.segment_sum(src, seg, n)
kernel_name = 'mk_perceiver_d1_seqx_r8_c9bd00'

def setup_inputs(seed: int=0):
    np.random.seed(seed)
    _w = jnp.asarray

    def _rec_inputs():
        import jax
        import jax.numpy as jnp
        _rk = jax.random.key(seed)
        x = 7.22e-05 + 1 * jax.random.normal(jax.random.fold_in(_rk, 1), (16, 32, 512), jnp.float32)
        _lenS = 32 - jax.random.randint(jax.random.fold_in(_rk, 7), (16,), 0, max(1, 32 // 4) + 1, jnp.int32)
        _lenS2 = 512 - jax.random.randint(jax.random.fold_in(_rk, 8), (16,), 0, max(1, 512 // 4) + 1, jnp.int32)
        _ctx_4096P = jax.random.normal(jax.random.fold_in(_rk, 11), (16, 16, 512), jnp.float32)
        _ctx_4096c = jax.random.dirichlet(jax.random.fold_in(_rk, 511), 0.3 * jnp.ones((16,), jnp.float32), (16, 512))
        _ctx_4096t = jnp.einsum('bsk,bkd->bsd', _ctx_4096c, _ctx_4096P)
        _ctx_4096t = _ctx_4096t * jax.lax.rsqrt(jnp.mean(jnp.square(_ctx_4096t)) + 1e-12) * 0.953939
        ctx_4096 = 4.13588e-05 + 0.999923 * (_ctx_4096t + 0.3 * jax.random.normal(jax.random.fold_in(_rk, 611), (16, 512, 512), jnp.float32))
        return (x, ctx_4096)
    x, ctx_4096 = _rec_inputs()

    def _L0_xattn_setup():
        import jax, jax.numpy as jnp
        import numpy as np
        DIM = 512
        NUM_HEADS = 32
        NUM_KV_HEADS = 8
        HEAD_DIM = DIM // NUM_HEADS
        KV_DIM = DIM // (NUM_HEADS // NUM_KV_HEADS)
        B, S = (1, 256)
        key = jax.random.key(seed)
        ks = jax.random.split(key, 7)
        w_scale = DIM ** (-0.5)
        return {'query': jax.random.normal(ks[0], (B, S, DIM), jnp.float32), 'key': jax.random.normal(ks[1], (B, S, DIM), jnp.float32), 'value': jax.random.normal(ks[2], (B, S, DIM), jnp.float32), 'Wq': jax.random.normal(ks[3], (DIM, DIM), jnp.float32) * w_scale, 'Wk': jax.random.normal(ks[4], (DIM, KV_DIM), jnp.float32) * w_scale, 'Wv': jax.random.normal(ks[5], (DIM, KV_DIM), jnp.float32) * w_scale, 'Wo': jax.random.normal(ks[6], (DIM, DIM), jnp.float32) * w_scale}
    _L0_xattn_all = _L0_xattn_setup()
    _L0_xattn_in = {k: v for k, v in _L0_xattn_all.items() if k in ('Wq', 'Wk', 'Wv', 'Wo')}
    del _L0_xattn_all

    def _L0_attn_setup():
        import jax, jax.numpy as jnp
        import numpy as np
        HIDDEN = 512
        NHQ = 32
        NHKV = 8
        HEAD_DIM = HIDDEN // NHQ
        THETA = 10000.0

        def _rope(x, theta_base):
            b, h, s, d = x.shape
            inv_freq = 1.0 / theta_base ** (jnp.arange(0, d, 2, dtype=jnp.float32)[:d // 2] / d)
            freqs = jnp.arange(s, dtype=jnp.float32)[:, None] * inv_freq[None, :]
            cos = jnp.cos(freqs).astype(x.dtype)
            sin = jnp.sin(freqs).astype(x.dtype)
            x1, x2 = (x[..., :d // 2], x[..., d // 2:])
            return jnp.concatenate([x1 * cos - x2 * sin, x2 * cos + x1 * sin], axis=-1)
        key = jax.random.key(seed)
        ks = jax.random.split(key, 5)
        std = 1.0 / np.sqrt(HIDDEN)
        x = jax.random.normal(ks[0], (2, 256, HIDDEN), dtype=jnp.float32)
        Wq = jax.random.normal(ks[1], (HIDDEN, HIDDEN), dtype=jnp.float32) * std
        Wk = jax.random.normal(ks[2], (HIDDEN, NHKV * HEAD_DIM), dtype=jnp.float32) * std
        Wv = jax.random.normal(ks[3], (HIDDEN, NHKV * HEAD_DIM), dtype=jnp.float32) * std
        Wo = jax.random.normal(ks[4], (HIDDEN, HIDDEN), dtype=jnp.float32) * std
        return {'x': x, 'Wq': Wq, 'Wk': Wk, 'Wv': Wv, 'Wo': Wo}
    _L0_attn_all = _L0_attn_setup()
    _L0_attn_in = {k: v for k, v in _L0_attn_all.items() if k in ('Wq', 'Wk', 'Wv', 'Wo')}
    del _L0_attn_all

    def _L0_ffn_setup():
        import jax, jax.numpy as jnp
        import numpy as np
        GROUP_SIZE = 32
        OUT_FEATURES = 512
        IN_FEATURES = 512

        def _unpack_3bit(p):
            b0, b1, b2 = (p[..., 0], p[..., 1], p[..., 2])
            v0 = b0 & 7
            v1 = b0 >> 3 & 7
            v2 = b0 >> 6 & 3 | (b1 & 1) << 2
            v3 = b1 >> 1 & 7
            v4 = b1 >> 4 & 7
            v5 = b1 >> 7 & 1 | (b2 & 3) << 1
            v6 = b2 >> 2 & 7
            v7 = b2 >> 5 & 7
            return jnp.stack([v0, v1, v2, v3, v4, v5, v6, v7], axis=-1)

        def _block_dequantize_3bit(packed, normalization, group_size=GROUP_SIZE):
            p = packed.astype(jnp.uint8).reshape(-1, group_size // 8, 3)
            q = _unpack_3bit(p).reshape(-1, group_size).astype(jnp.float32)
            n = normalization.astype(jnp.float32)
            x_norm = q / 7.0
            return (x_norm * (2.0 * n) - n).reshape(-1)
        key = jax.random.key(seed)
        k1, k2, k3, k4 = jax.random.split(key, 4)
        n_groups = OUT_FEATURES * IN_FEATURES // GROUP_SIZE
        packed_cols = GROUP_SIZE * 3 // 8
        x = jax.random.normal(k1, (2, 256, IN_FEATURES), dtype=jnp.float32)
        weight_q3 = jax.random.randint(k2, (n_groups, packed_cols), 0, 32, dtype=jnp.int32).astype(jnp.int8)
        weight_norm = jax.random.uniform(k3, (n_groups, 1), dtype=jnp.float32, minval=0.05, maxval=1.0)
        bias = jax.random.normal(k4, (OUT_FEATURES,), dtype=jnp.float32) * 0.02
        return {'x': x, 'weight_q3': weight_q3, 'weight_norm': weight_norm, 'bias': bias}
    _L0_ffn_all = _L0_ffn_setup()
    _L0_ffn_in = {k: v for k, v in _L0_ffn_all.items() if k in ('weight_q3', 'weight_norm', 'bias')}
    del _L0_ffn_all
    return {'x': x, 'ctx_4096': ctx_4096, 'L0_xattn_Wq': _L0_xattn_in['Wq'], 'L0_xattn_Wk': _L0_xattn_in['Wk'], 'L0_xattn_Wv': _L0_xattn_in['Wv'], 'L0_xattn_Wo': _L0_xattn_in['Wo'], 'L0_attn_Wq': _L0_attn_in['Wq'], 'L0_attn_Wk': _L0_attn_in['Wk'], 'L0_attn_Wv': _L0_attn_in['Wv'], 'L0_attn_Wo': _L0_attn_in['Wo'], 'L0_ffn_weight_q3': _L0_ffn_in['weight_q3'], 'L0_ffn_weight_norm': _L0_ffn_in['weight_norm'], 'L0_ffn_bias': _L0_ffn_in['bias']}

def reference(x, ctx_4096, L0_xattn_Wq, L0_xattn_Wk, L0_xattn_Wv, L0_xattn_Wo, L0_attn_Wq, L0_attn_Wk, L0_attn_Wv, L0_attn_Wo, L0_ffn_weight_q3, L0_ffn_weight_norm, L0_ffn_bias):
    import jax
    import jax.numpy as jnp

    def _L0_xattn_ref(query, key, value, Wq, Wk, Wv, Wo):
        import jax, jax.numpy as jnp
        import numpy as np
        DIM = 512
        NUM_HEADS = 32
        NUM_KV_HEADS = 8
        HEAD_DIM = DIM // NUM_HEADS
        KV_DIM = DIM // (NUM_HEADS // NUM_KV_HEADS)
        B, S = (1, 256)
        b, sq, _ = query.shape
        _, sk, _ = key.shape
        rep = NUM_HEADS // NUM_KV_HEADS
        q = (query @ Wq).reshape(b, sq, NUM_HEADS, HEAD_DIM).transpose(0, 2, 1, 3)
        k = (key @ Wk).reshape(b, sk, NUM_KV_HEADS, HEAD_DIM).transpose(0, 2, 1, 3)
        v = (value @ Wv).reshape(b, sk, NUM_KV_HEADS, HEAD_DIM).transpose(0, 2, 1, 3)
        k = jnp.repeat(k, rep, axis=1)
        v = jnp.repeat(v, rep, axis=1)
        scale = HEAD_DIM ** (-0.5)
        scores = jnp.einsum('bhqd,bhkd->bhqk', q, k) * scale
        probs = jax.nn.softmax(scores, axis=-1)
        out = jnp.einsum('bhqk,bhkd->bhqd', probs, v)
        out = out.transpose(0, 2, 1, 3).reshape(b, sq, DIM)
        return out @ Wo

    def _L0_attn_ref(x, Wq, Wk, Wv, Wo):
        import jax, jax.numpy as jnp
        import numpy as np
        HIDDEN = 512
        NHQ = 32
        NHKV = 8
        HEAD_DIM = HIDDEN // NHQ
        THETA = 10000.0

        def _rope(x, theta_base):
            b, h, s, d = x.shape
            inv_freq = 1.0 / theta_base ** (jnp.arange(0, d, 2, dtype=jnp.float32)[:d // 2] / d)
            freqs = jnp.arange(s, dtype=jnp.float32)[:, None] * inv_freq[None, :]
            cos = jnp.cos(freqs).astype(x.dtype)
            sin = jnp.sin(freqs).astype(x.dtype)
            x1, x2 = (x[..., :d // 2], x[..., d // 2:])
            return jnp.concatenate([x1 * cos - x2 * sin, x2 * cos + x1 * sin], axis=-1)
        b, s, _ = x.shape
        q_per_kv = NHQ // NHKV
        q = (x @ Wq).reshape(b, s, NHQ, HEAD_DIM).transpose(0, 2, 1, 3)
        k = (x @ Wk).reshape(b, s, NHKV, HEAD_DIM).transpose(0, 2, 1, 3)
        v = (x @ Wv).reshape(b, s, NHKV, HEAD_DIM).transpose(0, 2, 1, 3)
        q = _rope(q, THETA)
        k = _rope(k, THETA)
        qg = q.reshape(b, NHKV, q_per_kv, s, HEAD_DIM)
        scores = jnp.einsum('bkgqd,bkmd->bkgqm', qg, k) / np.sqrt(HEAD_DIM)
        causal = jnp.tril(jnp.ones((s, s), dtype=bool))
        scores = jnp.where(causal, scores, -jnp.inf)
        attn = jax.nn.softmax(scores, axis=-1)
        out = jnp.einsum('bkgqm,bkmd->bkgqd', attn, v)
        out = out.reshape(b, NHQ, s, HEAD_DIM).transpose(0, 2, 1, 3).reshape(b, s, HIDDEN)
        return out @ Wo

    def _L0_ffn_ref(x, weight_q3, weight_norm, bias):
        import jax, jax.numpy as jnp
        import numpy as np
        GROUP_SIZE = 32
        OUT_FEATURES = 512
        IN_FEATURES = 512

        def _unpack_3bit(p):
            b0, b1, b2 = (p[..., 0], p[..., 1], p[..., 2])
            v0 = b0 & 7
            v1 = b0 >> 3 & 7
            v2 = b0 >> 6 & 3 | (b1 & 1) << 2
            v3 = b1 >> 1 & 7
            v4 = b1 >> 4 & 7
            v5 = b1 >> 7 & 1 | (b2 & 3) << 1
            v6 = b2 >> 2 & 7
            v7 = b2 >> 5 & 7
            return jnp.stack([v0, v1, v2, v3, v4, v5, v6, v7], axis=-1)

        def _block_dequantize_3bit(packed, normalization, group_size=GROUP_SIZE):
            p = packed.astype(jnp.uint8).reshape(-1, group_size // 8, 3)
            q = _unpack_3bit(p).reshape(-1, group_size).astype(jnp.float32)
            n = normalization.astype(jnp.float32)
            x_norm = q / 7.0
            return (x_norm * (2.0 * n) - n).reshape(-1)
        w = _block_dequantize_3bit(weight_q3, weight_norm).reshape(OUT_FEATURES, IN_FEATURES)
        return jnp.einsum('bsi,oi->bso', x, w) + bias
    x = x + _L0_xattn_ref(_layernorm(x, axis=-1), ctx_4096, ctx_4096, L0_xattn_Wq, L0_xattn_Wk, L0_xattn_Wv, L0_xattn_Wo)
    x = x + _L0_attn_ref(_layernorm(x, axis=-1), L0_attn_Wq, L0_attn_Wk, L0_attn_Wv, L0_attn_Wo)
    x = x + _L0_ffn_ref(_layernorm(x, axis=-1), L0_ffn_weight_q3, L0_ffn_weight_norm, L0_ffn_bias)
    return x

_drawn_inputs = setup_inputs


def setup_inputs(seed=0):
    import zlib

    import numpy as np

    out = dict(_drawn_inputs(seed))
    spreads = {}
    factors = {'L0_ffn_bias': 27.014}
    for name, (base, spread) in spreads.items():
        noise = np.random.default_rng([zlib.crc32(name.encode()), seed]).standard_normal(out[name].shape)
        drawn = base * np.exp(spread * noise) if base else spread * noise
        out[name] = jnp.asarray(drawn.astype(out[name].dtype))
    for name, factor in factors.items():
        out[name] = (out[name] * factor).astype(out[name].dtype)
    return out
```

```python
from contextlib import ExitStack

import numpy as np

import concourse.bass as bass
from concourse import mybir
from concourse.alu_op_type import AluOpType as ALU

F32 = mybir.dt.float32
F32R = mybir.dt.float32r
BF16 = mybir.dt.bfloat16
I32 = mybir.dt.int32
U8 = mybir.dt.uint8
ACT = mybir.ActivationFunctionType
AX = mybir.AxisListType.X

P = 128
B, S, D, KEYS = 16, 32, 512, 512
HEADS, G, HD = 32, 8, 16
R = HEADS // G
KV = G * HD
C = D // P
KT = KEYS // P
TOK = B * S
TILES = TOK // P
BPT = P // S
GS = 32
SCALE = float(HD) ** -0.5
EPS = 1e-5
MASKED = -1e30
NGRP = D * TILES // GS
NTRIP = NGRP * GS // 8

K_PART = (0, 0, 0, 1, 1, 2)
Q_PART = (0, 1, 2, 0, 1, 0)
SLOTS = len(K_PART)
STACK = SLOTS * HD
HALF = G // 2
MROWS = 3 * HALF
ROWS = STACK + MROWS
VW = 2 * HD


def constants():
    inv = (1.0 / np.float32(10000.0) ** (np.arange(0, HD, 2, dtype=np.float32)[: HD // 2] / np.float32(HD))).astype(np.float32)
    ang = np.arange(S, dtype=np.float32)[:, None] * inv[None, :]
    cos, sin = np.cos(ang).astype(np.float32), np.sin(ang).astype(np.float32)
    rope = np.stack([np.concatenate([cos, cos], 1), np.concatenate([-sin, sin], 1)], 1)
    rope = np.tile(rope, (P // S, 1, 1)).astype(np.float32)
    t = np.arange(P) % S
    causal = np.where(np.arange(S)[None, :] <= t[:, None], 0.0, MASKED).astype(np.float32)
    group_of_row = (np.arange(P)[:, None] // HD == np.arange(G)[None, :]).astype(np.float32)
    batch_of_row = (np.arange(P)[:, None] // S == np.arange(BPT)[None, :]).astype(np.float32)
    pair = 0x3F803F80
    sel = np.zeros((MROWS, G, KEYS // 2), np.int32)
    for row in range(MROWS):
        sel[row, np.arange(G) % HALF == row % HALF] = pair
    return {"rope": rope, "causal": causal, "group_mask": group_of_row, "batch_mask": batch_of_row,
            "sel": sel, "ident": np.eye(P, dtype=np.float32)}


def perceiver(nc, x_d, ctx_d, xwq_d, xwk_d, xwv_d, xwo_d, swq_d, swk_d, swv_d, swo_d, q3_d, norm_d, bias_d,
              rope_d, causal_d, group_mask_d, batch_mask_d, sel_d, ident_d, out_d):
    kscr = nc.dram_tensor("kscr", [2, SLOTS, KV, KEYS], BF16).ap()
    qscr = nc.dram_tensor("qscr", [B, SLOTS, KV, P], BF16).ap()
    xf = x_d.rearrange("b s d -> (b s) d").rearrange("(t p) d -> p t d", p=P)
    of = out_d.rearrange("b s d -> (b s) d").rearrange("(t p) d -> t p d", p=P)

    with ExitStack() as ctx:
        def sb(name, shape, dt=F32):
            return ctx.enter_context(nc.sbuf_tensor(name, shape, dt))

        def sem(name):
            return ctx.enter_context(nc.semaphore(name))

        ident = sb("ident_sb", [P, P])
        ident_h = sb("ident_h", [P, P], BF16)
        rope = sb("rope_sb", [P, 2, HD])
        causal = sb("causal_sb", [P, S])
        group_mask = sb("group_mask_sb", [P, G])
        batch_mask = sb("batch_mask_sb", [P, BPT])
        bias = sb("bias_sb", [P, D])
        wkv_raw = sb("wkv_raw", [P, 2, C, KV])
        wkv_h = sb("wkv_h", [P, 2, C, KV], F32R)
        wkv_l = sb("wkv_l", [P, 2, C, KV], F32R)
        wo = sb("wo", [P, R, D])
        swq = sb("swq", [P, C, D])
        wT = sb("wT", [P, C, D])
        cx = sb("cx", [P, 2, KT, D])
        cT_h = sb("cT_h", [P, C, KEYS], F32R)
        cT_l = sb("cT_l", [P, C, KEYS], F32R)
        kparts = sb("kparts", [P, 2, 3, KEYS], BF16)
        kres = sb("kres", [P, 2, KEYS])
        vT = sb("vT", [P, KEYS])
        vaug = sb("vaug", [P, 4, KT, G, VW])
        kstack = sb("kstack", [P, 4, G, KEYS], BF16)
        qstack = sb("qstack", [P, 4, G, P], BF16)
        zeros = sb("zeros", [P, KEYS], BF16)
        negmax = sb("negmax", [P, 2, G])
        maxres = sb("maxres", [P, 2, HALF])
        mparts = sb("mparts", [P, 2, 3, HALF], BF16)
        rden = sb("rden", [P, 2, G])
        o_raw = sb("o_raw", [P, 2, P])
        o_sb = sb("o_sb", [P, 2, G, HD])
        oT = sb("oT", [P, TILES, R, P])
        xs = sb("xs", [P, TILES, D])
        st = sb("st", [P, TILES, 6])
        mv = sb("mv", [P, TILES, 2])
        rstd = sb("rstd", [P, TILES])
        q3 = sb("q3_sb", [P, TILES, D // GS * 3], I32)
        wnorm = sb("wnorm", [P, 2, NGRP])

        region = sb("region", [P, 11264])

        def carve(sizes):
            at, parts = 0, []
            for size in sizes:
                parts.append(region[:, at:at + size])
                at += size
            assert at <= 11264
            return parts

        xwq, xhT, xh, qparts, wnat = carve((2048, 2048, 2048, 3072, 2048))
        pT = region[:, 0:G * KT * P].rearrange("p (g a n) -> p g a n", g=G, a=KT)
        xwq = xwq.rearrange("p (c n) -> p c n", c=C)
        xhT = xhT.rearrange("p (c n) -> p c n", c=C)
        xh = xh.rearrange("p (t n) -> p t n", t=TILES)
        qparts = qparts.bitcast(BF16).rearrange("p (k b r t) -> p k b r t", k=3, b=B, r=R)
        x1, xn, xnT, rot_a, rot_b, kbd, _, swkv, swo, q2T, sm, vbd, o2, o2T, p2 = carve(
            (512, 512, 512, 640, 640, 1024, 256, 1024, 2048, 512, 512, 512, 512, 512, 1024))
        swkv = swkv.rearrange("p (c n) -> p c n", c=C)
        swo = swo.rearrange("p (r n) -> p r n", r=R)
        xnT = xnT.rearrange("p (c n) -> p c n", c=C)
        q2T = q2T.rearrange("p (b n) -> p b n", b=BPT)
        kbd = kbd.rearrange("p (b g k) -> p b g k", b=BPT, g=G)
        sm = sm.rearrange("p (b g k) -> p b g k", b=2, g=G)
        vbd = vbd.rearrange("p (g b d) -> p g b d", g=G, b=BPT)
        o2 = o2.rearrange("p (b g d) -> p b g d", b=BPT, g=G)
        o2T = o2T.rearrange("p (r b t) -> p r b t", r=R, b=BPT)
        p2 = p2.rearrange("p (g b k) -> p g b k", g=G, b=BPT)
        pT2 = wkv_raw[:].rearrange("p i c n -> p (i c n)").rearrange("p (g n) -> p g n", g=G)
        q_rot = rot_a[:, 0:D]
        k_rot = rot_a[:, D:D + KV]
        smax = sb("smax", [P, 2, G])
        ssum = sb("ssum", [P, G, BPT])

        scratch = kstack[:, 2:4].rearrange("p a g n -> p (a g n)").bitcast(F32)
        qbytes = scratch[:, 0:3 * NTRIP].bitcast(I32).rearrange("p (n k) -> p n k", k=3)
        qvals = scratch[:, 3 * NTRIP:11 * NTRIP].bitcast(I32).rearrange("p (n k) -> p n k", k=8)
        wq_dg = kstack[:, 0].rearrange("p g n -> p (g n)").bitcast(F32).rearrange("p (c r n) -> p c r n", c=C, r=R)
        bits = scratch[:, 11 * NTRIP:15 * NTRIP].bitcast(I32).rearrange("p (k n) -> p k n", k=4)

        def bank(name):
            return ctx.enter_context(nc.psum_tensor(name, [P, 512], F32))

        b_t = bank("b_t")
        b_x = bank("b_x")
        b_k = bank("b_k")
        b_v = bank("b_v")
        b_s = bank("b_s")
        b_c = [bank(f"b_c{i}") for i in range(2)]
        b_d = bank("b_d")
        b_y = b_t

        names = """wkv_loaded consts_loaded ident_loaded x_loaded xwq_loaded sel_loaded packed_loaded
            wkv_high wkv_split identh_ready ones_ready ctx_transposed ctx_high ctx_low k_summed v_chunk k_high k_res
            k_mid k_low vT_ready v_transposed v_ready s_ready max_ready mpart_high mpart_res mpart_mid mpart_ready
            m_transposed mrows_ready st_ready exp_ready pv_ready oraw_ready oraw_transposed rden_ready o_ready o_transposed oT_ready
            ln1_step ln1_var ln1_std xh_ready xh_transposed xhT_ready q_summed q_high q_res q_mid q_low
            wq_ordered zeros_ready unpack_step unpacked w_scaled w_step w_ready w_transposed wT_ready weights_loaded tail_weights_loaded
            wo_summed x1_ready ln_stats ln_aggr ln_var ln_std ln_rstd xn_ready xn_transposed xnT_ready
            sq_summed sq_turned q_rot_ready skv_summed sk_turned vbd_ready k_rot_ready q_transposed q2T_ready
            k_transposed kbd_ready ss_summed ss_masked smax_ready ss_shifted p2_ready ssum_ready rsum_ready
            p_transposed pT2_ready so_summed o2_ready o2_transposed o2T_ready swo_summed x2_ready x2b_ready
            ffn_summed out_ready out_stored"""
        sems = {name: sem(name) for name in names.split()}
        (wkv_loaded, consts_loaded, ident_loaded, x_loaded, xwq_loaded, sel_loaded, packed_loaded,
         wkv_high, wkv_split, identh_ready, ones_ready, ctx_transposed, ctx_high, ctx_low, k_summed, v_chunk, k_high, k_res,
         k_mid, k_low, vT_ready, v_transposed, v_ready, s_ready, max_ready, mpart_high, mpart_res, mpart_mid, mpart_ready,
         m_transposed, mrows_ready, st_ready, exp_ready, pv_ready, oraw_ready, oraw_transposed, rden_ready, o_ready, o_transposed, oT_ready,
         ln1_step, ln1_var, ln1_std, xh_ready, xh_transposed, xhT_ready, q_summed, q_high, q_res, q_mid, q_low,
         wq_ordered, zeros_ready, unpack_step, unpacked, w_scaled, w_step, w_ready, w_transposed, wT_ready, weights_loaded, tail_weights_loaded,
         wo_summed, x1_ready, ln_stats, ln_aggr, ln_var, ln_std, ln_rstd, xn_ready, xn_transposed, xnT_ready,
         sq_summed, sq_turned, q_rot_ready, skv_summed, sk_turned, vbd_ready, k_rot_ready, q_transposed, q2T_ready,
         k_transposed, kbd_ready, ss_summed, ss_masked, smax_ready, ss_shifted, p2_ready, ssum_ready, rsum_ready,
         p_transposed, pT2_ready, so_summed, o2_ready, o2_transposed, o2T_ready, swo_summed, x2_ready, x2b_ready,
         ffn_summed, out_ready, out_stored) = (sems[name] for name in names.split())
        ctx_loaded = [sem(f"ctx_loaded{i}") for i in range(2)]
        k_stored = [sem(f"k_stored{i}") for i in range(2)]
        kstack_loaded = [sem(f"kstack_loaded{i}") for i in range(4)]
        qstack_loaded = [sem(f"qstack_loaded{i}") for i in range(4)]
        q_stored = [sem(f"q_stored{t}") for t in range(TILES)]

        FIRST, LAST, TRIPS = -2, B + 1, 3

        def slots(eng, slot, start, between=None):
            for n in range(FIRST, start):
                slot(n, 0)
                if between is not None:
                    between(n)
            with eng.Fori(0, TRIPS) as trip:
                for n in range(start, start + 4):
                    slot(n, trip)
            for n in range(start + 4 * TRIPS, LAST + 1):
                slot(n, 0)

        def looped(trip):
            return not isinstance(trip, int)

        def live(m, trip):
            return looped(trip) or 0 <= m < B

        def wait(eng, semaphore, per, m, extra, trip):
            base = per * m + extra
            if looped(trip):
                assert base >= 0
                eng.wait_ge(semaphore, 4 * per * trip + base)
            elif base > 0:
                eng.wait_ge(semaphore, base)

        def wait_ring(eng, semaphores, m, trip, dmas=1):
            ring = len(semaphores)
            base = 16 * dmas * (m // ring + 1)
            if looped(trip):
                eng.wait_ge(semaphores[m % ring], 16 * dmas * (4 // ring) * trip + base)
            elif m >= 0:
                eng.wait_ge(semaphores[m % ring], base)

        def count(eng, semaphore, value):
            if value > 0:
                eng.wait_ge(semaphore, value)

        block = ctx.enter_context(nc.Block())

        @block.sync
        def _(sp):
            for i, w in enumerate((xwk_d, xwv_d)):
                sp.dma_start(wkv_raw[:, i], w.rearrange("(c p) m -> p c m", p=P)).then_inc(wkv_loaded, 16)

            def load_ctx(m, trip):
                sp.dma_start(cx[:, m % 2], ctx_d[4 * trip + m].rearrange("(p a) d -> p a d", a=KT)).then_inc(ctx_loaded[m % 2], 16)

            def load_qstack(m, trip):
                sp.dma_start(qstack[0:STACK, m % 4],
                             qscr[4 * trip + m].rearrange("s (d g) n -> (s d) g n", g=G)).then_inc(qstack_loaded[m % 4], 16)

            load_ctx(0, 0)
            sp.dma_start(xs[:], xf).then_inc(x_loaded, 16)
            sp.dma_start(xwq, xwq_d.rearrange("(c p) n -> p c n", p=P)).then_inc(xwq_loaded, 16)

            def slot(n, trip):
                m = n + 1
                if looped(trip):
                    through, transposed, split, stored = (
                        sp.snap(step * trip + base) for step, base in
                        ((4 * G, G * (n - 1) + 1), (4 * C, C * m + C), (4, m + 1), (32 * SLOTS, 16 * SLOTS * (m // 2 + 1))))
                else:
                    through, transposed, split, stored = G * (n - 1) + 1, C * m + C, m + 1, 16 * SLOTS * (m // 2 + 1)
                if live(m, trip):
                    if looped(trip) or n >= 1:
                        sp.wait_ge(st_ready, through)
                    sp.wait_ge(k_high, split)
                    sp.wait_ge(k_low, split)
                    for s, part in enumerate(K_PART):
                        sp.dma_start(kscr[m % 2, s], kparts[:, m % 2, part]).then_inc(k_stored[m % 2], 16)
                if live(n + 3, trip):
                    if looped(trip) or m >= 0:
                        sp.wait_ge(ctx_transposed, transposed)
                    load_ctx(n + 3, trip)
                if live(m, trip):
                    sp.wait_ge(k_stored[m % 2], stored)
                    if not looped(trip) and m == 0:
                        sp.wait_ge(q_summed, R)
                    if not looped(trip) and m in (2, 3):
                        sp.wait_ge(unpacked, 1)
                    sp.dma_start(kstack[0:STACK, m % 4],
                                 kscr[m % 2].rearrange("s (d g) n -> (s d) g n", g=G)).then_inc(kstack_loaded[m % 4], 16)
                    if looped(trip) or m > 0:
                        load_qstack(m, trip)

            def between(n):
                if n == -1:
                    sp.wait_ge(q_high, R)
                    sp.wait_ge(q_low, R)
                    for t in range(TILES):
                        bs = slice(BPT * t, BPT * t + BPT)
                        for s, part in enumerate(Q_PART):
                            sp.dma_start(qscr[bs, s].rearrange("b p n -> p b n"),
                                         qparts[:, part, bs].rearrange("p b r t -> p b (r t)")).then_inc(q_stored[t], 16)
                        if t == 0:
                            sp.wait_ge(q_stored[0], 16 * SLOTS)
                            load_qstack(0, 0)
                if n == 0:
                    for t in range(1, TILES):
                        sp.wait_ge(q_stored[t], 16 * SLOTS)
                    sp.dma_start(swkv[:, :, 0:KV], swk_d.rearrange("(c p) n -> p c n", p=P)).then_inc(tail_weights_loaded, 16)
                    sp.dma_start(swkv[:, :, KV:2 * KV], swv_d.rearrange("(c p) n -> p c n", p=P)).then_inc(tail_weights_loaded, 16)
                    for g in range(G):
                        sp.dma_start(swo[HD * g:HD * g + HD],
                                     swo_d[R * HD * g:R * HD * (g + 1)].rearrange("(r d) n -> d r n", r=R)).then_inc(tail_weights_loaded, 16)

            slots(sp, slot, 1, between)
            for t in range(TILES):
                sp.wait_ge(out_ready, t + 1)
                sp.dma_start(of[t], xn).then_inc(out_stored, 16)
            sp.wait_ge(out_stored, 16 * TILES)

        @block.gpsimd
        def _(pool):
            nc.gpsimd.memset(vaug[:, :, :, :, HD:VW], 1.0).then_inc(ones_ready, 1)

            nc.gpsimd.memset(zeros[:], 0.0).then_inc(zeros_ready, 1)
            pool.wait_ge(zeros_ready, 1)
            pool.wait_ge(xwq_loaded, 16)
            for c in range(C):
                nc.gpsimd.tensor_copy(wq_dg[:, c].rearrange("p r (d g) -> p r d g", g=G),
                                      xwq[:, c].rearrange("p (g r d) -> p r d g", g=G, r=R)).then_inc(wq_ordered, 1)

            def key_parts(m, trip):
                wait(pool, k_res, 1, m, 1, trip)
                wait_ring(pool, k_stored, m - 2, trip, SLOTS)
                nc.gpsimd.tensor_tensor(kparts[:, m % 2, 1], kres[:, m % 2], zeros[:], ALU.add).then_inc(k_mid, 1)
                wait(pool, k_mid, 1, m, 1, trip)
                nc.gpsimd.tensor_tensor(kparts[:, m % 2, 2], kres[:, m % 2], kparts[:, m % 2, 1], ALU.subtract).then_inc(k_low, 1)

            def max_parts(m, half, trip):
                nm = negmax[:, m % 2, HALF * half:HALF * half + HALF]
                wait(pool, max_ready, G, m, HALF * (half + 1), trip)
                wait(pool, m_transposed, 2, m - 1, half + 1, trip)
                nc.gpsimd.tensor_tensor(mparts[:, half, 0], nm, zeros[:, 0:HALF], ALU.add).then_inc(mpart_high, 1)
                wait(pool, mpart_high, 2, m, half + 1, trip)
                nc.gpsimd.tensor_tensor(maxres[:, half], nm, mparts[:, half, 0], ALU.subtract).then_inc(mpart_res, 1)
                wait(pool, mpart_res, 2, m, half + 1, trip)
                nc.gpsimd.tensor_tensor(mparts[:, half, 1], maxres[:, half], zeros[:, 0:HALF], ALU.add).then_inc(mpart_mid, 1)
                wait(pool, mpart_mid, 2, m, half + 1, trip)
                nc.gpsimd.tensor_tensor(mparts[:, half, 2], maxres[:, half], mparts[:, half, 1], ALU.subtract).then_inc(mpart_ready, 1)

            def slot(n, trip):
                if live(n - 1, trip):
                    max_parts(n - 1, 1, trip)
                if live(n + 1, trip):
                    key_parts(n + 1, trip)
                if live(n, trip):
                    max_parts(n, 0, trip)

            def between(n):
                if n == -2:
                    for r in range(R):
                        res = xh[:, r].rearrange("p (b t) -> p b t", t=S)
                        pool.wait_ge(q_res, r + 1)
                        nc.gpsimd.tensor_copy(qparts[:, 1, :, r], res).then_inc(q_mid, 1)
                        pool.wait_ge(q_mid, r + 1)
                        nc.gpsimd.tensor_tensor(qparts[:, 2, :, r], res, qparts[:, 1, :, r], ALU.subtract).then_inc(q_low, 1)
                if n == -1:
                    wide = wnat.rearrange("p (n k) -> p n k", k=GS)
                    pool.wait_ge(packed_loaded, 32)
                    nc.gpsimd.tensor_scalar(wnorm[:, 1], wnorm[:, 0], 2.0, None, ALU.mult).then_inc(w_scaled, 1)
                    pool.wait_ge(w_scaled, 1)
                    pool.wait_ge(unpacked, 1)
                    nc.gpsimd.tensor_tensor(wide, wide, wnorm[:, 1].unsqueeze(2).to_broadcast([P, NGRP, GS]), ALU.mult).then_inc(w_step, 1)
                    pool.wait_ge(w_step, 1)
                    nc.gpsimd.tensor_tensor(wide, wide, wnorm[:, 0].unsqueeze(2).to_broadcast([P, NGRP, GS]), ALU.subtract).then_inc(w_ready, 1)

            slots(pool, slot, 2, between)

            pool.wait_ge(consts_loaded, 80)
            for t in range(TILES):
                pool.wait_ge(sq_turned, t + 1)
                rot = (rot_a[:, 0:D], rot_b[:, 0:D])
                nc.gpsimd.tensor_tensor(q_rot, rot[0], rot[1], ALU.add).then_inc(q_rot_ready, 1)
                pool.wait_ge(sk_turned, t + 1)
                nc.gpsimd.tensor_tensor(k_rot, k_rot, rot_b[:, D:D + KV], ALU.add).then_inc(k_rot_ready, 1)
                for half in range(2):
                    k = 2 * t + half
                    pool.wait_ge(smax_ready, k + 1)
                    nc.gpsimd.tensor_tensor(sm, sm, smax[:].unsqueeze(3).to_broadcast([P, 2, G, S]), ALU.subtract).then_inc(ss_shifted, 1)
                pool.wait_ge(xn_ready, 2 * t + 2)
                nc.gpsimd.tensor_tensor(x1, x1, bias[:], ALU.add).then_inc(x2b_ready, 1)

        @block.scalar
        def _(act):
            act.dma_start(ident[:], ident_d).then_inc(ident_loaded, 16)
            act.dma_start(q3[:], q3_d.rearrange("(t p g) k -> p t (g k)", t=TILES, p=P)).then_inc(packed_loaded, 16)
            act.dma_start(wnorm[:, 0].rearrange("p (t g) -> p t g", t=TILES),
                          norm_d.rearrange("(t p g) a -> p t (g a)", t=TILES, p=P)).then_inc(packed_loaded, 16)
            act.dma_start(kstack[STACK:ROWS, 1].bitcast(I32), sel_d).then_inc(sel_loaded, 16)
            for dst, src in ((rope, rope_d), (causal, causal_d), (group_mask, group_mask_d), (batch_mask, batch_mask_d)):
                act.dma_start(dst[:], src).then_inc(consts_loaded, 16)
            act.dma_start(bias[:], bias_d.partition_broadcast(P)).then_inc(consts_loaded, 16)
            act.wait_ge(wkv_loaded, 32)
            nc.scalar.activation(wkv_h[:, 0].rearrange("p c (d g) -> p c d g", g=G),
                                 wkv_raw[:, 0].rearrange("p c (g d) -> p c d g", g=G), ACT.Copy).then_inc(wkv_high, 1)
            nc.scalar.activation(wkv_h[:, 1], wkv_raw[:, 1], ACT.Copy).then_inc(wkv_high, 1)
            act.wait_ge(ident_loaded, 16)
            nc.scalar.activation(ident_h[:], ident[:], ACT.Copy).then_inc(identh_ready, 1)

            def max_rows(m, half, trip):
                wait(act, m_transposed, 2, m, half + 1, trip)
                nc.scalar.activation(qstack[STACK:ROWS, m % 4, HALF * half:HALF * half + HALF],
                                     b_x[STACK:ROWS, 0:P // 2].bitcast(BF16).unsqueeze(1).to_broadcast([MROWS, HALF, P]),
                                     ACT.Copy).then_inc(mrows_ready, 1)

            def slot(n, trip):
                for g in range(G):
                    if g == 0 and live(n + 1, trip):
                        m = n + 1
                        wait(act, k_summed, 1, m, 1, trip)
                        wait_ring(act, k_stored, m - 2, trip, SLOTS)
                        nc.scalar.activation(kparts[:, m % 2, 0], b_k[:], ACT.Copy).then_inc(k_high, 1)
                    if g == 1 and live(n + 1, trip):
                        m = n + 1
                        wait(act, v_chunk, C, m, C, trip)
                        wait(act, v_transposed, 1, m, 0, trip)
                        nc.scalar.activation(vT[:], b_v[:], ACT.Copy).then_inc(vT_ready, 1)
                    if g % 2 == 0 and live(n + 2, trip):
                        m, c = n + 2, g // 2
                        wait(act, ctx_transposed, C, m, c + 1, trip)
                        wait(act, v_chunk, C, m - 1, c + 1, trip)
                        nc.scalar.activation(cT_h[:, c], b_t[:], ACT.Copy).then_inc(ctx_high, 1)
                    if live(n - 1, trip):
                        m = n - 1
                        wait(act, st_ready, G, m, g + 1, trip)
                        wait(act, pv_ready, 2, m - 1, g // HALF + 1, trip)
                        nc.scalar.activation(pT[:, g], b_c[g % 2][:].rearrange("p (a n) -> p a n", a=KT),
                                             ACT.Exp, scale=SCALE).then_inc(exp_ready, 1)
                    if g == 2 and live(n - 1, trip):
                        max_rows(n - 1, 1, trip)
                    if g == 2 and live(n - 2, trip):
                        m = n - 2
                        wait(act, pv_ready, 2, m, 2, trip)
                        wait(act, oraw_transposed, 1, m, 0, trip)
                        nc.scalar.activation(o_raw[:], b_d[:, 0:2 * P].rearrange("p (h n) -> p h n", h=2), ACT.Copy).then_inc(oraw_ready, 1)
                    if g == 7 and live(n, trip):
                        max_rows(n, 0, trip)
                    if n == B - 2 and g < C:
                        act.wait_ge(w_transposed, g + 1)
                        nc.scalar.activation(wT[:, g], b_y[:], ACT.Copy).then_inc(wT_ready, 1)

            def between(n):
                if n == -2:
                    act.wait_ge(ln1_var, 1)
                    nc.scalar.activation(rstd[:], mv[:, :, 1], ACT.Sqrt).then_inc(ln1_std, 1)
                    for t in range(TILES):
                        act.wait_ge(xh_transposed, t + 1)
                        nc.scalar.activation(xhT[:, :, P * t:P * t + P], (b_x, b_s)[t % 2][:].rearrange("p (c n) -> p c n", c=C),
                                             ACT.Copy).then_inc(xhT_ready, 1)
                    for r in range(R):
                        act.wait_ge(q_summed, r + 1)
                        nc.scalar.activation(qparts[:, 0, :, r], b_c[r % 2][:].rearrange("p (b t) -> p b t", t=S),
                                             ACT.Copy).then_inc(q_high, 1)
                    for g in range(G):
                        act.dma_start(wo[HD * g:HD * g + HD],
                                      xwo_d[R * HD * g:R * HD * (g + 1)].rearrange("(r d) n -> d r n", r=R)).then_inc(weights_loaded, 16)
                    act.dma_start(swq[:], swq_d.rearrange("(c p) n -> p c n", p=P)).then_inc(weights_loaded, 16)
                    act.wait_ge(unpacked, 1)
                    for i in (0, 2, 3):
                        act.dma_start(kstack[STACK:ROWS, i].bitcast(I32), sel_d).then_inc(sel_loaded, 16)

            slots(act, slot, 2, between)

            for t in range(TILES):
                for norm in range(2):
                    k = 2 * t + norm
                    if norm == 1:
                        act.wait_ge(q_transposed, t + 1)
                        nc.scalar.activation(q2T.rearrange("p b (r t) -> p r b t", r=R),
                                             b_y[:].rearrange("p (r b t) -> p r b t", r=R, b=BPT), ACT.Copy).then_inc(q2T_ready, 1)
                        for half in range(2):
                            j = 2 * t + half
                            act.wait_ge(ss_shifted, j + 1)
                            nc.scalar.activation(p2[:, :, 2 * half:2 * half + 2].rearrange("p g b k -> p b g k"), sm,
                                                 ACT.Exp, scale=SCALE).then_inc(p2_ready, 1)
                        for half in range(2):
                            j = 2 * t + half
                            act.wait_ge(p_transposed, j + 1)
                            nc.scalar.activation(pT2[:, HALF * half:HALF * half + HALF],
                                                 b_y[:].rearrange("p (g n) -> p g n", g=HALF), ACT.Copy).then_inc(pT2_ready, 1)
                        act.wait_ge(o2_transposed, t + 1)
                        nc.scalar.activation(o2T.rearrange("p r b t -> p b r t"),
                                             b_y[:].rearrange("p (b r t) -> p b r t", b=BPT, r=R), ACT.Copy).then_inc(o2T_ready, 1)
                    act.wait_ge(ln_var, k + 1)
                    nc.scalar.activation(rstd[:, 0:1], mv[:, 0, 1:2], ACT.Sqrt).then_inc(ln_std, 1)
                    act.wait_ge(xn_transposed, k + 1)
                    nc.scalar.activation(xnT, b_y[:].rearrange("p (c n) -> p c n", c=C), ACT.Copy).then_inc(xnT_ready, 1)

        @block.vector
        def _(dve):
            dve.wait_ge(wkv_high, 2)
            nc.vector.tensor_tensor(wkv_l[:, 0].rearrange("p c (d g) -> p c d g", g=G),
                                    wkv_raw[:, 0].rearrange("p c (g d) -> p c d g", g=G),
                                    wkv_h[:, 0].rearrange("p c (d g) -> p c d g", g=G).bitcast(F32), ALU.subtract).then_inc(wkv_split, 1)
            nc.vector.tensor_tensor(wkv_l[:, 1], wkv_raw[:, 1], wkv_h[:, 1].bitcast(F32), ALU.subtract).then_inc(wkv_split, 1)

            def normalise(m, trip):
                acc = b_d[:, 2 * P:].rearrange("p (g v) -> p g v", v=VW)
                wait(dve, oraw_transposed, 1, m, 1, trip)
                nc.vector.reciprocal(rden[:, m % 2], acc[:, :, HD]).then_inc(rden_ready, 1)
                wait(dve, rden_ready, 1, m, 1, trip)
                nc.vector.tensor_tensor(o_sb[:, m % 2], acc[:, :, 0:HD],
                                        rden[:, m % 2].unsqueeze(2).to_broadcast([P, G, HD]), ALU.mult).then_inc(o_ready, 1)

            def slot(n, trip):
                for g in range(G):
                    if live(n, trip):
                        wait(dve, s_ready, G, n, g + 1, trip)
                        if g % HALF == 0:
                            wait(dve, mpart_res, 2, n - 2, g // HALF + 1, trip)
                        nc.vector.tensor_reduce(negmax[:, n % 2, g:g + 1], b_s[:], AX, ALU.max, negate=True).then_inc(max_ready, 1)
                    if g == 0 and live(n + 1, trip):
                        m = n + 1
                        wait(dve, k_high, 1, m, 1, trip)
                        wait(dve, k_low, 1, m - 2, 1, trip)
                        nc.vector.tensor_tensor(kres[:, m % 2], b_k[:], kparts[:, m % 2, 0], ALU.subtract).then_inc(k_res, 1)
                    if g == 4 and live(n + 1, trip):
                        m = n + 1
                        wait(dve, v_transposed, 1, m, 1, trip)
                        nc.vector.tensor_copy(vaug[:, m % 4, :, :, 0:HD],
                                              b_x[:].rearrange("p (a g d) -> p a g d", a=KT, g=G)).then_inc(v_ready, 1)
                    if g % 2 == 0 and live(n + 2, trip):
                        m, c = n + 2, g // 2
                        wait(dve, ctx_high, C, m, c + 1, trip)
                        nc.vector.tensor_tensor(cT_l[:, c], b_t[:], cT_h[:, c].bitcast(F32), ALU.subtract).then_inc(ctx_low, 1)
                    if g == 3 and live(n - 2, trip):
                        normalise(n - 2, trip)
                    if g == 5 and live(n - 2, trip):
                        m = n - 2
                        wait(dve, o_transposed, 1, m, 1, trip)
                        tile = m // BPT + trip
                        nc.vector.tensor_copy(oT[:, tile, :, S * (m % BPT):S * (m % BPT) + S],
                                              b_x[:, 0:P].rearrange("p (r t) -> p r t", r=R)).then_inc(oT_ready, 1)

            def between(n):
                if n == -2:
                    dve.wait_ge(x_loaded, 16)
                    for t in range(TILES):
                        nc.vector.bn_stats(st[:, t], xs[:, t]).then_inc(ln1_step, 1)
                    for t in range(TILES):
                        dve.wait_ge(ln1_step, t + 1)
                        nc.vector.bn_aggr(mv[:, t], st[:, t]).then_inc(ln1_step, 1)
                    dve.wait_ge(ln1_step, 2 * TILES)
                    nc.vector.tensor_scalar(mv[:, :, 1], mv[:, :, 1], EPS, None, ALU.add).then_inc(ln1_var, 1)
                    dve.wait_ge(ln1_std, 1)
                    nc.vector.reciprocal(rstd[:], rstd[:]).then_inc(ln1_step, 1)
                    dve.wait_ge(ln1_step, 2 * TILES + 1)
                    for t in range(TILES):
                        nc.vector.tensor_scalar(xh[:, t], xs[:, t], mv[:, t, 0:1], rstd[:, t:t + 1], ALU.subtract,
                                                ALU.mult).then_inc(xh_ready, 1)
                    for r in range(R):
                        dve.wait_ge(q_high, r + 1)
                        nc.vector.tensor_tensor(xh[:, r].rearrange("p (b t) -> p b t", t=S),
                                                b_c[r % 2][:].rearrange("p (b t) -> p b t", t=S),
                                                qparts[:, 0, :, r], ALU.subtract).then_inc(q_res, 1)
                    SHR, SHL, AND, OR = ALU.logical_shift_right, ALU.logical_shift_left, ALU.bitwise_and, ALU.bitwise_or
                    b0, b1, b2 = (qbytes[:, :, k] for k in range(3))
                    dve.wait_ge(packed_loaded, 32)
                    nc.vector.tensor_copy(qbytes.rearrange("p n k -> p (n k)"),
                                          q3[:].rearrange("p t n -> p (t n)").bitcast(U8)).then_inc(unpack_step, 1)
                    dve.wait_ge(unpack_step, 1)
                    nc.vector.tensor_scalar(bits[:, 0], b0, 6, 3, SHR, AND).then_inc(unpack_step, 1)
                    nc.vector.tensor_scalar(bits[:, 1], b1, 1, 2, AND, SHL).then_inc(unpack_step, 1)
                    nc.vector.tensor_scalar(bits[:, 2], b1, 7, 1, SHR, AND).then_inc(unpack_step, 1)
                    nc.vector.tensor_scalar(bits[:, 3], b2, 3, 1, AND, SHL).then_inc(unpack_step, 1)
                    for k, byte, shift in ((0, b0, 0), (1, b0, 3), (3, b1, 1), (4, b1, 4), (6, b2, 2), (7, b2, 5)):
                        nc.vector.tensor_scalar(qvals[:, :, k], byte, shift, 7, SHR, AND).then_inc(unpack_step, 1)
                    dve.wait_ge(unpack_step, 5)
                    nc.vector.tensor_tensor(qvals[:, :, 2], bits[:, 0], bits[:, 1], OR).then_inc(unpack_step, 1)
                    nc.vector.tensor_tensor(qvals[:, :, 5], bits[:, 2], bits[:, 3], OR).then_inc(unpack_step, 1)
                    dve.wait_ge(unpack_step, 13)
                    nc.vector.tensor_scalar(wnat, qvals.rearrange("p n k -> p (n k)"), 1.0 / 7.0, None, ALU.mult).then_inc(unpacked, 1)

            slots(dve, slot, 2, between)

            def layer_norm(k):
                if k % 2 == 0:
                    dve.wait_ge(x1_ready, k // 2 + 1)
                else:
                    dve.wait_ge(x2_ready, k // 2 + 1)
                nc.vector.bn_stats(st[:, 0], x1).then_inc(ln_stats, 1)
                dve.wait_ge(ln_stats, k + 1)
                nc.vector.bn_aggr(mv[:, 0], st[:, 0]).then_inc(ln_aggr, 1)
                dve.wait_ge(ln_aggr, k + 1)
                nc.vector.tensor_scalar(mv[:, 0, 1:2], mv[:, 0, 1:2], EPS, None, ALU.add).then_inc(ln_var, 1)
                dve.wait_ge(ln_std, k + 1)
                nc.vector.reciprocal(rstd[:, 0:1], rstd[:, 0:1]).then_inc(ln_rstd, 1)
                dve.wait_ge(ln_rstd, k + 1)
                nc.vector.tensor_scalar(xn, x1, mv[:, 0, 0:1], rstd[:, 0:1], ALU.subtract, ALU.mult).then_inc(xn_ready, 1)

            cos = rope[:, 0].unsqueeze(1)
            sin = rope[:, 1].unsqueeze(1)
            H2 = HD // 2

            def turn(psum, at, width, done):
                heads = width // HD
                a = rot_a[:, at:at + width]
                b = rot_b[:, at:at + width]
                if heads == HEADS:
                    src = psum.rearrange("p (g r d) -> p r g d", g=G, r=R)
                    a, b = (v.rearrange("p (r g d) -> p r g d", r=R, g=G) for v in (a, b))
                    cs, sn = (v.unsqueeze(1) for v in (cos, sin))
                    shape = lambda w: [P, R, G, w]
                else:
                    src, a, b = (v.rearrange("p (g d) -> p g d", g=G) for v in (psum, a, b))
                    cs, sn = cos, sin
                    shape = lambda w: [P, G, w]
                nc.vector.tensor_tensor(a, src, cs.to_broadcast(shape(HD)), ALU.mult)
                nc.vector.tensor_tensor(b[..., 0:H2], src[..., H2:HD], sn[..., 0:H2].to_broadcast(shape(H2)), ALU.mult)
                nc.vector.tensor_tensor(b[..., H2:HD], src[..., 0:H2], sn[..., H2:HD].to_broadcast(shape(H2)), ALU.mult).then_inc(done, 1)

            dve.wait_ge(consts_loaded, 80)
            for t in range(TILES):
                dve.wait_ge(wo_summed, t + 1)
                nc.vector.tensor_tensor(x1, b_y[:], xs[:, t], ALU.add).then_inc(x1_ready, 1)
                layer_norm(2 * t)
                dve.wait_ge(sq_summed, t + 1)
                turn(b_y[:], 0, D, sq_turned)
                dve.wait_ge(skv_summed, t + 1)
                turn(b_y[:, 0:KV], D, KV, sk_turned)
                nc.vector.tensor_tensor(vbd, b_y[:, KV:2 * KV].rearrange("p (g d) -> p g d", g=G).unsqueeze(2).to_broadcast([P, G, BPT, HD]),
                                        batch_mask[:].unsqueeze(1).unsqueeze(3).to_broadcast([P, G, BPT, HD]), ALU.mult).then_inc(vbd_ready, 1)
                dve.wait_ge(k_transposed, t + 1)
                nc.vector.tensor_tensor(kbd, b_y[:, 0:P].rearrange("p (b k) -> p b k", b=BPT).unsqueeze(2).to_broadcast([P, BPT, G, S]),
                                        group_mask[:].unsqueeze(1).unsqueeze(3).to_broadcast([P, BPT, G, S]), ALU.mult).then_inc(kbd_ready, 1)
                for half in range(2):
                    k = 2 * t + half
                    dve.wait_ge(ss_summed, k + 1)
                    count(dve, p2_ready, k)
                    nc.vector.tensor_tensor(sm.rearrange("p b g k -> p (b g) k"), b_y[:].rearrange("p (n k) -> p n k", k=S),
                                            causal[:].unsqueeze(1).to_broadcast([P, 2 * G, S]), ALU.add).then_inc(ss_masked, 1)
                    dve.wait_ge(ss_masked, k + 1)
                    nc.vector.tensor_reduce(smax[:], sm, AX, ALU.max).then_inc(smax_ready, 1)
                dve.wait_ge(p2_ready, 2 * t + 2)
                nc.vector.tensor_reduce(ssum[:], p2, AX, ALU.add).then_inc(ssum_ready, 1)
                dve.wait_ge(ssum_ready, t + 1)
                nc.vector.reciprocal(ssum[:], ssum[:]).then_inc(rsum_ready, 1)
                dve.wait_ge(rsum_ready, t + 1)
                dve.wait_ge(so_summed, t + 1)
                nc.vector.tensor_tensor(o2.rearrange("p b g d -> p g b d"), b_y[:].rearrange("p (g b d) -> p g b d", g=G, b=BPT),
                                        ssum[:].unsqueeze(3).to_broadcast([P, G, BPT, HD]), ALU.mult).then_inc(o2_ready, 1)
                dve.wait_ge(swo_summed, t + 1)
                nc.vector.tensor_tensor(x1, b_y[:], x1, ALU.add).then_inc(x2_ready, 1)
                layer_norm(2 * t + 1)
                dve.wait_ge(x2b_ready, t + 1)
                dve.wait_ge(ffn_summed, t + 1)
                nc.vector.tensor_tensor(xn, b_y[:], x1, ALU.add).then_inc(out_ready, 1)
                dve.wait_ge(out_stored, 16 * t + 16)

        @block.tensor
        def _(pe):
            def ctx_chunk(m, c, trip):
                if c == 0:
                    wait_ring(pe, ctx_loaded, m, trip)
                wait(pe, ctx_low, C, m, c, trip)
                for a in range(KT):
                    last = nc.tensor.transpose(b_t[:, P * a:P * a + P], cx[:, m % 2, a, P * c:P * c + P], ident[:])
                last.then_inc(ctx_transposed, 1)

            def project(m, which, c, trip):
                wait(pe, ctx_low, C, m, c + 1, trip)
                if c == 0:
                    wait(pe, vT_ready if which else k_res, 1, m, 0, trip)
                out = (b_k, b_v)[which][:]
                nc.tensor.matmul(out, wkv_h[:, which, c], cT_h[:, c], start=(c == 0), stop=False)
                nc.tensor.matmul(out, wkv_l[:, which, c], cT_h[:, c], start=False, stop=False)
                last = nc.tensor.matmul(out, wkv_h[:, which, c], cT_l[:, c], start=False, stop=(c == C - 1))
                if which == 1:
                    last.then_inc(v_chunk, 1)
                elif c == C - 1:
                    last.then_inc(k_summed, 1)

            def max_rows(m, half, trip):
                wait(pe, mpart_ready, 2, m, half + 1, trip)
                nc.tensor.transpose(b_x[STACK:ROWS, 0:P // 2].bitcast(BF16),
                                    mparts[:, half].rearrange("p k j -> p (k j)"), ident_h[:]).then_inc(m_transposed, 1)

            def times_v(m, half, trip):
                wait(pe, exp_ready, G, m, HALF * (half + 1), trip)
                if half == 0:
                    wait(pe, v_ready, 1, m, 1, trip)
                    wait(pe, o_ready, 1, m, 0, trip)
                for a in range(KT):
                    for j in range(HALF):
                        g = HALF * half + j
                        last = nc.tensor.matmul(b_d[VW * j:VW * j + VW, P * half:P * half + P], vaug[:, m % 4, a, g],
                                                pT[:, g, a], start=(a == 0), stop=(a == KT - 1))
                last.then_inc(pv_ready, 1)

            def slot(n, trip):
                for g in range(G):
                    if live(n, trip):
                        if g == 0:
                            wait_ring(pe, kstack_loaded, n, trip)
                            wait_ring(pe, qstack_loaded, n, trip)
                        wait(pe, max_ready, G, n, g, trip)
                        nc.tensor.matmul(b_s[:], qstack[0:STACK, n % 4, g], kstack[0:STACK, n % 4, g],
                                         start=True, stop=True).then_inc(s_ready, 1)
                    if g % 2 == 0 and live(n + 2, trip):
                        ctx_chunk(n + 2, g // 2, trip)
                    if live(n - 1, trip):
                        m = n - 1
                        wait(pe, exp_ready, G, m, g - 1, trip)
                        if g % HALF == 0:
                            wait(pe, mrows_ready, 2, m, g // HALF + 1, trip)
                        for a in range(KT):
                            last = nc.tensor.matmul(b_c[g % 2][:, P * a:P * a + P], kstack[0:ROWS, m % 4, g, P * a:P * a + P],
                                                    qstack[0:ROWS, m % 4, g], start=True, stop=True)
                        last.then_inc(st_ready, 1)
                    if g == 1 and live(n - 2, trip):
                        times_v(n - 2, 1, trip)
                    if g == 6 and live(n - 1, trip):
                        times_v(n - 1, 0, trip)
                    if g == 2 and live(n - 1, trip):
                        wait(pe, mrows_ready, 2, n - 1, 1, trip)
                        max_rows(n - 1, 1, trip)
                    if g == 3 and live(n + 1, trip):
                        m = n + 1
                        wait(pe, vT_ready, 1, m, 1, trip)
                        if live(n - 1, trip):
                            wait(pe, mrows_ready, 2, n - 1, 2, trip)
                        for a in range(KT):
                            last = nc.tensor.transpose(b_x[:, P * a:P * a + P], vT[:, P * a:P * a + P], ident[:])
                        last.then_inc(v_transposed, 1)
                    if g == 3 and live(n - 2, trip):
                        m = n - 2
                        wait(pe, oraw_ready, 1, m, 1, trip)
                        for half in range(2):
                            last = nc.tensor.transpose(b_d[:, P * (2 + half):P * (3 + half)], o_raw[:, half], ident[:])
                        last.then_inc(oraw_transposed, 1)
                    if g == 5 and live(n - 2, trip):
                        m = n - 2
                        if live(n + 1, trip):
                            wait(pe, v_ready, 1, n + 1, 1, trip)
                        elif live(n - 1, trip):
                            wait(pe, mrows_ready, 2, n - 1, 2, trip)
                        wait(pe, o_ready, 1, m, 1, trip)
                        nc.tensor.transpose(b_x[:, 0:P], o_sb[:, m % 2].rearrange("p g d -> p (g d)"), ident[:]).then_inc(o_transposed, 1)
                    if g == 6 and live(n, trip):
                        if live(n + 1, trip):
                            wait(pe, v_ready, 1, n + 1, 1, trip)
                        if live(n - 2, trip):
                            wait(pe, oT_ready, 1, n - 2, 1, trip)
                        if not looped(trip) and n == 0:
                            pe.wait_ge(identh_ready, 1)
                            pe.wait_ge(sel_loaded, 64)
                        max_rows(n, 0, trip)
                    if n == B - 2 and g < C:
                        pe.wait_ge(w_ready, 1)
                        pe.wait_ge(ctx_low, C * B)
                        count(pe, wT_ready, g)
                        for t in range(TILES):
                            at = D * t + P * g
                            last = nc.tensor.transpose(b_y[:, P * t:P * t + P], wnat[:, at:at + P], ident[:])
                        last.then_inc(w_transposed, 1)
                    if not looped(trip) and n == -2 and g == 1:
                        pe.wait_ge(wkv_split, 2)
                    if g % 2 and live(n + 2, trip):
                        project(n + 2, 0, g // 2, trip)
                    if g == 0 and live(n + 1, trip):
                        project(n + 1, 1, C - 1, trip)
                    if g in (2, 4, 6) and live(n + 2, trip):
                        project(n + 2, 1, g // 2 - 1, trip)

            def between(n):
                if n == -2:
                    for t in range(TILES):
                        pe.wait_ge(xh_ready, t + 1)
                        count(pe, xhT_ready, t - 1)
                        for c in range(C):
                            last = nc.tensor.transpose((b_x, b_s)[t % 2][:, P * c:P * c + P], xh[:, t, P * c:P * c + P], ident[:])
                        last.then_inc(xh_transposed, 1)
                    pe.wait_ge(xhT_ready, TILES)
                    pe.wait_ge(wq_ordered, C)
                    for r in range(R):
                        count(pe, q_res, r - 1)
                        for c in range(C):
                            last = nc.tensor.matmul(b_c[r % 2][:], wq_dg[:, c, r], xhT[:, c], start=(c == 0), stop=(c == C - 1))
                        last.then_inc(q_summed, 1)
                    pe.wait_ge(q_res, R)

            pe.wait_ge(ident_loaded, 16)
            slots(pe, slot, 2, between)

            pe.wait_ge(oT_ready, B)
            pe.wait_ge(weights_loaded, 16 * (G + 1))
            pe.wait_ge(tail_weights_loaded, 16 * (G + 2))

            def rows_by(lhsT, weight, chunks, done, out=b_y):
                for c in range(chunks):
                    last = nc.tensor.matmul(out, lhsT(c), weight(c), start=(c == 0), stop=(c == chunks - 1))
                last.then_inc(done, 1)

            def transpose_rows(k):
                pe.wait_ge(xn_ready, k + 1)
                for c in range(C):
                    last = nc.tensor.transpose(b_y[:, P * c:P * c + P], xn[:, P * c:P * c + P], ident[:])
                last.then_inc(xn_transposed, 1)
                pe.wait_ge(xnT_ready, k + 1)

            for t in range(TILES):
                count(pe, out_ready, t)
                rows_by(lambda r: oT[:, t, r], lambda r: wo[:, r], R, wo_summed, b_y[:])
                transpose_rows(2 * t)
                rows_by(lambda c: xnT[:, c], lambda c: swq[:, c], C, sq_summed, b_y[:])
                pe.wait_ge(sq_turned, t + 1)
                rows_by(lambda c: xnT[:, c], lambda c: swkv[:, c], C, skv_summed, b_y[:, 0:2 * KV])
                pe.wait_ge(q_rot_ready, t + 1)
                pe.wait_ge(vbd_ready, t + 1)
                for r in range(R):
                    last = nc.tensor.transpose(b_y[:, P * r:P * r + P], q_rot[:, P * r:P * r + P], ident[:])
                last.then_inc(q_transposed, 1)
                pe.wait_ge(k_rot_ready, t + 1)
                pe.wait_ge(q2T_ready, t + 1)
                nc.tensor.transpose(b_y[:, 0:P], k_rot, ident[:]).then_inc(k_transposed, 1)
                pe.wait_ge(kbd_ready, t + 1)
                for half in range(2):
                    if half:
                        pe.wait_ge(ss_masked, 2 * t + 1)
                    for b in range(2):
                        last = nc.tensor.matmul(b_y[:, G * S * b:G * S * (b + 1)], q2T[:, 2 * half + b],
                                                kbd[:, 2 * half + b].rearrange("p g k -> p (g k)"), start=True, stop=True)
                    last.then_inc(ss_summed, 1)
                pe.wait_ge(p2_ready, 2 * t + 2)
                for half in range(2):
                    if half:
                        pe.wait_ge(pT2_ready, 2 * t + 1)
                    for g in range(HALF):
                        last = nc.tensor.transpose(b_y[:, P * g:P * g + P], p2[:, HALF * half + g].rearrange("p b k -> p (b k)"), ident[:])
                    last.then_inc(p_transposed, 1)
                pe.wait_ge(pT2_ready, 2 * t + 2)
                for g in range(G):
                    last = nc.tensor.matmul(b_y[:, BPT * HD * g:BPT * HD * (g + 1)], pT2[:, g],
                                            vbd[:, g].rearrange("p b d -> p (b d)"), start=True, stop=True)
                last.then_inc(so_summed, 1)
                pe.wait_ge(o2_ready, t + 1)
                for b in range(BPT):
                    last = nc.tensor.transpose(b_y[:, P * b:P * b + P], o2[:, b].rearrange("p g d -> p (g d)"), ident[:])
                last.then_inc(o2_transposed, 1)
                pe.wait_ge(o2T_ready, t + 1)
                rows_by(lambda r: o2T[:, r].rearrange("p b t -> p (b t)"), lambda r: swo[:, r], R, swo_summed, b_y[:])
                transpose_rows(2 * t + 1)
                pe.wait_ge(wT_ready, C)
                rows_by(lambda c: xnT[:, c], lambda c: wT[:, c], C, ffn_summed, b_y[:])


_INS = ["x", "ctx_4096", "L0_xattn_Wq", "L0_xattn_Wk", "L0_xattn_Wv", "L0_xattn_Wo", "L0_attn_Wq", "L0_attn_Wk",
        "L0_attn_Wv", "L0_attn_Wo", "L0_ffn_weight_q3", "L0_ffn_weight_norm", "L0_ffn_bias"]


def kernel(**inputs):
    import numpy as _np
    import concourse.bacc as _bacc
    from concourse import mybir as _mybir
    from concourse.bass_utils import run_bass_kernel_spmd as _run

    nc = _bacc.Bacc("TRN2", target_bir_lowering=False, num_devices=1)
    arrays = {name: _np.ascontiguousarray(inputs[name]) for name in _INS}
    arrays["L0_ffn_weight_q3"] = arrays["L0_ffn_weight_q3"].view(_np.int32)
    arrays.update(constants())
    args = []
    feeds = {}
    for name, a in arrays.items():
        feeds[f"in_{name}_dram"] = a
        args.append(nc.dram_tensor(f"in_{name}_dram", a.shape, _mybir.dt.from_np(a.dtype), kind="ExternalInput").ap())
    out = nc.dram_tensor("out_dram", (B, S, D), F32, kind="ExternalOutput").ap()
    perceiver(nc, *args, out)
    r = _run(nc, [feeds], core_ids=[0])
    return r.results[0]["out_dram"]
```

```python
from contextlib import ExitStack

import numpy as np

import concourse.bass as bass
from concourse import mybir
from concourse.alu_op_type import AluOpType as ALU

F32 = mybir.dt.float32
F32R = mybir.dt.float32r
BF16 = mybir.dt.bfloat16
I32 = mybir.dt.int32
U8 = mybir.dt.uint8
ACT = mybir.ActivationFunctionType
AX = mybir.AxisListType.X

P = 128
B, S, D, KEYS = 16, 32, 512, 512
HEADS, G, HD = 32, 8, 16
R = HEADS // G
KV = G * HD
C = D // P
KT = KEYS // P
TOK = B * S
TILES = TOK // P
BPT = P // S
GS = 32
SCALE = float(HD) ** -0.5
EPS = 1e-5
MASKED = -1e30
NGRP = D * TILES // GS
NTRIP = NGRP * GS // 8

STEPS = ("residual1", "normalise1", "transpose1", "queries", "keys_values", "heads_to_columns", "spread_values",
         "scores", "probabilities", "transpose_probabilities", "attend", "residual2", "normalise2", "transpose2", "feed_forward")
SKEW = 2
EARLY = {(14, 5): ("residual1", 0), (14, 7): ("normalise1", 0), (15, 0): ("transpose1", 0), (15, 2): ("queries", 0),
         (15, 5): ("keys_values", 0), (16, 0): ("residual1", 1), (16, 2): ("normalise1", 1), (16, 4): ("transpose1", 1),
         (16, 6): ("queries", 1), (17, 0): ("residual1", 2), (17, 1): ("keys_values", 1), (17, 3): ("normalise1", 2),
         (17, 5): ("transpose1", 2)}
LATE = [(step, t) for _, t, step in sorted((SKEW * t + i, t, step) for t in range(TILES) for i, step in enumerate(STEPS))
        if (step, t) not in EARLY.values()]

K_PART = (0, 0, 0, 1, 1, 2)
Q_PART = (0, 1, 2, 0, 1, 0)
SLOTS = len(K_PART)
STACK = SLOTS * HD
HALF = G // 2
MROWS = 3 * HALF
ROWS = STACK + MROWS
VW = 2 * HD


def constants():
    inv = (1.0 / np.float32(10000.0) ** (np.arange(0, HD, 2, dtype=np.float32)[: HD // 2] / np.float32(HD))).astype(np.float32)
    ang = np.arange(S, dtype=np.float32)[:, None] * inv[None, :]
    cos, sin = np.cos(ang).astype(np.float32), np.sin(ang).astype(np.float32)
    rope = np.stack([np.concatenate([cos, cos], 1), np.concatenate([-sin, sin], 1)], 1)
    rope = np.tile(rope, (P // S, 1, 1)).astype(np.float32)
    t = np.arange(P) % S
    causal = np.where(np.arange(2 * G * S)[None, :] % S <= t[:, None], 0.0, MASKED).astype(np.float32)
    causal = np.ascontiguousarray((causal.view(np.uint32) >> 16).astype(np.uint16)).view(np.int32)
    group_of_row = (np.arange(P)[:, None] // HD == np.arange(G)[None, :]).astype(np.float32)
    batch_of_row = (np.arange(P)[:, None] // S == np.arange(BPT)[None, :]).astype(np.float32)
    pair = 0x3F803F80
    sel = np.zeros((MROWS, G, KEYS // 2), np.int32)
    for row in range(MROWS):
        sel[row, np.arange(G) % HALF == row % HALF] = pair
    return {"rope": rope, "causal": causal, "group_mask": group_of_row, "batch_mask": batch_of_row,
            "sel": sel, "ident": np.eye(P, dtype=np.float32)}


def perceiver(nc, x_d, ctx_d, xwq_d, xwk_d, xwv_d, xwo_d, swq_d, swk_d, swv_d, swo_d, q3_d, norm_d, bias_d,
              rope_d, causal_d, group_mask_d, batch_mask_d, sel_d, ident_d, out_d):
    kscr = nc.dram_tensor("kscr", [2, SLOTS, KV, KEYS], BF16).ap()
    qscr = nc.dram_tensor("qscr", [B, SLOTS, KV, P], BF16).ap()
    xf = x_d.rearrange("b s d -> (b s) d").rearrange("(t p) d -> p t d", p=P)
    of = out_d.rearrange("b s d -> (b s) d").rearrange("(t p) d -> t p d", p=P)

    with ExitStack() as ctx:
        def sb(name, shape, dt=F32):
            return ctx.enter_context(nc.sbuf_tensor(name, shape, dt))

        def sem(name):
            return ctx.enter_context(nc.semaphore(name))

        ident = sb("ident_sb", [P, P])
        ident_h = sb("ident_h", [P, P], BF16)
        rope = sb("rope_sb", [P, 2, HD])
        causal = sb("causal_sb", [P, 2 * G * S], BF16)
        group_mask = sb("group_mask_sb", [P, G])
        batch_mask = sb("batch_mask_sb", [P, BPT])
        bias = sb("bias_sb", [P, D])
        wkv_raw = sb("wkv_raw", [P, 2, C, KV])
        wkv_h = sb("wkv_h", [P, 2, C, KV], F32R)
        wkv_l = sb("wkv_l", [P, 2, C, KV], F32R)
        wo = sb("wo", [P, R, D])
        swq = sb("swq", [P, C, D])
        wT = sb("wT", [P, C, D])
        cx = sb("cx", [P, 2, KT, D])
        cT_h = sb("cT_h", [P, C, KEYS], F32R)
        cT_l = sb("cT_l", [P, C, KEYS], F32R)
        kparts = sb("kparts", [P, 2, 3, KEYS], BF16)
        kres = sb("kres", [P, 2, KEYS])
        vT = sb("vT", [P, KEYS])
        vaug = sb("vaug", [P, 4, KT, G, VW])
        kstack = sb("kstack", [P, 4, G, KEYS], BF16)
        qstack = sb("qstack", [P, 4, G, P], BF16)
        zeros = sb("zeros", [P, KEYS], BF16)
        negmax = sb("negmax", [P, 2, G])
        maxres = sb("maxres", [P, 2, HALF])
        mparts = sb("mparts", [P, 2, 3, HALF], BF16)
        rden = sb("rden", [P, 2, G])
        o_raw = sb("o_raw", [P, 2, P])
        o_sb = sb("o_sb", [P, 2, G, HD])
        oT = sb("oT", [P, TILES, R, P])
        xs = sb("xs", [P, TILES, D])
        st = sb("st", [P, TILES, 6])
        mv = sb("mv", [P, TILES, 2])
        rstd = sb("rstd", [P, TILES])
        q3 = sb("q3_sb", [P, TILES, D // GS * 3], I32)
        wnorm = sb("wnorm", [P, 2, NGRP])

        region = sb("region", [P, 11264])

        def carve(sizes):
            at, parts = 0, []
            for size in sizes:
                parts.append(region[:, at:at + size])
                at += size
            assert at <= 11264
            return parts

        xwq, xhT, xh, qparts, wnat = carve((2048, 2048, 2048, 3072, 2048))
        pT = region[:, 0:G * KT * P].rearrange("p (g a n) -> p g a n", g=G, a=KT)
        xwq = xwq.rearrange("p (c n) -> p c n", c=C)
        xhT = xhT.rearrange("p (c n) -> p c n", c=C)
        xh = xh.rearrange("p (t n) -> p t n", t=TILES)
        qparts = qparts.bitcast(BF16).rearrange("p (k b r t) -> p k b r t", k=3, b=B, r=R)
        swkv, swo = region[:, 4096:5120], region[:, 5120:7168]
        swkv = swkv.rearrange("p (c n) -> p c n", c=C)
        swo = swo.rearrange("p (r n) -> p r n", r=R)
        by_tile = lambda words: words.rearrange("p (t n) -> p t n", t=TILES)
        xn = by_tile(region[:, 7168:9216])
        rotq_b = region[:, 9216:10240].rearrange("p (i n) -> p i n", i=2)
        k_rot = by_tile(region[:, 10240:10752])
        v2 = by_tile(region[:, 10752:11264])
        old_cx = cx[:].rearrange("p i a d -> p (i a d)")
        old_raw = wkv_raw[:].rearrange("p i c n -> p (i c n)")
        old_kstack = kstack[:].rearrange("p i g n -> p (i g n)").bitcast(F32)
        xnT = by_tile(old_cx[:, 0:2048]).rearrange("p t (c n) -> p t c n", c=C)
        o2T = by_tile(old_cx[:, 0:2048]).rearrange("p t (r b n) -> p t r b n", r=R, b=BPT)
        q_rot = by_tile(old_cx[:, 2048:4096])
        rotk_b = by_tile(old_raw[:, 0:512])
        k2T = by_tile(old_raw[:, 512:1024])
        kbd = by_tile(region[:, 0:4096]).rearrange("p t (b g k) -> p t b g k", b=BPT, g=G)
        p2 = by_tile(old_kstack[:, 0:4096]).rearrange("p t (b g k) -> p t b g k", b=BPT, g=G)
        pT2 = by_tile(old_kstack[:, 4096:8192]).rearrange("p t (b h n) -> p t b h n", b=BPT, h=2)
        old_vaug = vaug[:].rearrange("p i a g d -> p (i a g d)")
        vbd = by_tile(old_vaug[:, 0:2048]).rearrange("p t (b n) -> p t b n", b=BPT)
        q2T = by_tile(old_vaug[:, 2048:4096]).rearrange("p t (b n) -> p t b n", b=BPT)
        spread = kres[:].rearrange("p i n -> p (i n)")[:, 0:BPT * P].rearrange("p (b j k) -> p b j k", b=BPT, j=HALF)
        smax = sb("smax", [P, TILES, BPT, G])
        ssum = sb("ssum", [P, TILES, BPT, G])

        scratch = kstack[:, 2:4].rearrange("p a g n -> p (a g n)").bitcast(F32)
        qbytes = scratch[:, 0:3 * NTRIP].bitcast(I32).rearrange("p (n k) -> p n k", k=3)
        qvals = scratch[:, 3 * NTRIP:11 * NTRIP].bitcast(I32).rearrange("p (n k) -> p n k", k=8)
        wq_dg = kstack[:, 0].rearrange("p g n -> p (g n)").bitcast(F32).rearrange("p (c r n) -> p c r n", c=C, r=R)
        bits = scratch[:, 11 * NTRIP:15 * NTRIP].bitcast(I32).rearrange("p (k n) -> p k n", k=4)

        def bank(name):
            return ctx.enter_context(nc.psum_tensor(name, [P, 512], F32))

        b_t = bank("b_t")
        b_x = bank("b_x")
        b_k = bank("b_k")
        b_v = bank("b_v")
        b_s = bank("b_s")
        b_c = [bank(f"b_c{i}") for i in range(2)]
        b_d = bank("b_d")
        b_y = b_t
        bank_x, bank_y = (b_k, b_t, b_c[0], b_x), (b_v, b_s, b_c[1], b_d)

        names = """wkv_loaded consts_loaded ident_loaded x_loaded xwq_loaded sel_loaded packed_loaded
            wkv_high wkv_split identh_ready ones_ready ctx_transposed ctx_high ctx_low k_summed v_chunk k_high k_res
            k_mid k_low vT_ready v_transposed v_ready s_ready max_ready mpart_high mpart_res mpart_mid mpart_ready
            m_transposed mrows_ready st_ready exp_ready pv_ready oraw_ready oraw_transposed rden_ready o_ready o_transposed oT_ready
            ln1_step ln1_var ln1_std xh_ready xh_transposed xhT_ready q_summed q_high q_res q_mid q_low
            wq_ordered zeros_ready unpack_step unpacked w_scaled w_step w_ready w_transposed wT_ready weights_loaded tail_weights_loaded
            wo_summed x1_ready xn_transposed xnT_ready
            sq_summed sq_turned q_rot_ready skv_summed sk_turned v2_ready k_rot_ready q_transposed q2T_ready spread_ready
            v_spread vbd_ready k_transposed k2T_ready kbd_ready ss_summed smax_ready ss_shifted p2_ready ssum_ready rsum_ready
            p2_scaled p_transposed pT2_ready so_summed o2T_ready swo_summed x2_ready xn2_transposed xnT2_ready x2b_ready
            ffn_summed out_ready out_stored"""
        sems = {name: sem(name) for name in names.split()}
        (wkv_loaded, consts_loaded, ident_loaded, x_loaded, xwq_loaded, sel_loaded, packed_loaded,
         wkv_high, wkv_split, identh_ready, ones_ready, ctx_transposed, ctx_high, ctx_low, k_summed, v_chunk, k_high, k_res,
         k_mid, k_low, vT_ready, v_transposed, v_ready, s_ready, max_ready, mpart_high, mpart_res, mpart_mid, mpart_ready,
         m_transposed, mrows_ready, st_ready, exp_ready, pv_ready, oraw_ready, oraw_transposed, rden_ready, o_ready, o_transposed, oT_ready,
         ln1_step, ln1_var, ln1_std, xh_ready, xh_transposed, xhT_ready, q_summed, q_high, q_res, q_mid, q_low,
         wq_ordered, zeros_ready, unpack_step, unpacked, w_scaled, w_step, w_ready, w_transposed, wT_ready, weights_loaded, tail_weights_loaded,
         wo_summed, x1_ready, xn_transposed, xnT_ready,
         sq_summed, sq_turned, q_rot_ready, skv_summed, sk_turned, v2_ready, k_rot_ready, q_transposed, q2T_ready, spread_ready,
         v_spread, vbd_ready, k_transposed, k2T_ready, kbd_ready, ss_summed, smax_ready, ss_shifted, p2_ready, ssum_ready, rsum_ready,
         p2_scaled, p_transposed, pT2_ready, so_summed, o2T_ready, swo_summed, x2_ready, xn2_transposed, xnT2_ready, x2b_ready,
         ffn_summed, out_ready, out_stored) = (sems[name] for name in names.split())
        ln_stats, ln_aggr, ln_var, ln_std, ln_rstd, xn_ready = (
            [sem(f"{name}{i + 1}") for i in range(2)] for name in ("ln_stats", "ln_aggr", "ln_var", "ln_std", "ln_rstd", "xn_ready"))
        ctx_loaded = [sem(f"ctx_loaded{i}") for i in range(2)]
        k_stored = [sem(f"k_stored{i}") for i in range(2)]
        kstack_loaded = [sem(f"kstack_loaded{i}") for i in range(4)]
        qstack_loaded = [sem(f"qstack_loaded{i}") for i in range(4)]
        q_stored = [sem(f"q_stored{t}") for t in range(TILES)]

        FIRST, LAST, TRIPS = -2, B + 1, 3

        def slots(eng, slot, start, between=None):
            for n in range(FIRST, start):
                slot(n, 0)
                if between is not None:
                    between(n)
            with eng.Fori(0, TRIPS) as trip:
                for n in range(start, start + 4):
                    slot(n, trip)
            for n in range(start + 4 * TRIPS, LAST + 1):
                slot(n, 0)

        def looped(trip):
            return not isinstance(trip, int)

        def live(m, trip):
            return looped(trip) or 0 <= m < B

        def wait(eng, semaphore, per, m, extra, trip):
            base = per * m + extra
            if looped(trip):
                assert base >= 0
                eng.wait_ge(semaphore, 4 * per * trip + base)
            elif base > 0:
                eng.wait_ge(semaphore, base)

        def wait_ring(eng, semaphores, m, trip, dmas=1):
            ring = len(semaphores)
            base = 16 * dmas * (m // ring + 1)
            if looped(trip):
                eng.wait_ge(semaphores[m % ring], 16 * dmas * (4 // ring) * trip + base)
            elif m >= 0:
                eng.wait_ge(semaphores[m % ring], base)

        def count(eng, semaphore, value):
            if value > 0:
                eng.wait_ge(semaphore, value)

        def early(n, g, steps):
            if (n, g) in EARLY:
                step, t = EARLY[n, g]
                steps[step](t)

        def late(steps):
            for step, t in LATE:
                steps[step](t)

        block = ctx.enter_context(nc.Block())

        @block.sync
        def _(sp):
            for i, w in enumerate((xwk_d, xwv_d)):
                sp.dma_start(wkv_raw[:, i], w.rearrange("(c p) m -> p c m", p=P)).then_inc(wkv_loaded, 16)

            def load_ctx(m, trip):
                sp.dma_start(cx[:, m % 2], ctx_d[4 * trip + m].rearrange("(p a) d -> p a d", a=KT)).then_inc(ctx_loaded[m % 2], 16)

            def load_qstack(m, trip):
                sp.dma_start(qstack[0:STACK, m % 4],
                             qscr[4 * trip + m].rearrange("s (d g) n -> (s d) g n", g=G)).then_inc(qstack_loaded[m % 4], 16)

            load_ctx(0, 0)
            sp.dma_start(xs[:], xf).then_inc(x_loaded, 16)
            sp.dma_start(xwq, xwq_d.rearrange("(c p) n -> p c n", p=P)).then_inc(xwq_loaded, 16)

            def slot(n, trip):
                m = n + 1
                if looped(trip):
                    through, transposed, split, stored = (
                        sp.snap(step * trip + base) for step, base in
                        ((4 * G, G * (n - 1) + 1), (4 * C, C * m + C), (4, m + 1), (32 * SLOTS, 16 * SLOTS * (m // 2 + 1))))
                else:
                    through, transposed, split, stored = G * (n - 1) + 1, C * m + C, m + 1, 16 * SLOTS * (m // 2 + 1)
                if live(m, trip):
                    if looped(trip) or n >= 1:
                        sp.wait_ge(st_ready, through)
                    sp.wait_ge(k_high, split)
                    sp.wait_ge(k_low, split)
                    for s, part in enumerate(K_PART):
                        sp.dma_start(kscr[m % 2, s], kparts[:, m % 2, part]).then_inc(k_stored[m % 2], 16)
                if live(n + 3, trip):
                    if looped(trip) or m >= 0:
                        sp.wait_ge(ctx_transposed, transposed)
                    load_ctx(n + 3, trip)
                if live(m, trip):
                    sp.wait_ge(k_stored[m % 2], stored)
                    if not looped(trip) and m == 0:
                        sp.wait_ge(q_summed, R)
                    if not looped(trip) and m in (2, 3):
                        sp.wait_ge(unpacked, 1)
                    sp.dma_start(kstack[0:STACK, m % 4],
                                 kscr[m % 2].rearrange("s (d g) n -> (s d) g n", g=G)).then_inc(kstack_loaded[m % 4], 16)
                    if looped(trip) or m > 0:
                        load_qstack(m, trip)

            def between(n):
                if n == -1:
                    sp.wait_ge(q_high, R)
                    sp.wait_ge(q_low, R)
                    for t in range(TILES):
                        bs = slice(BPT * t, BPT * t + BPT)
                        for s, part in enumerate(Q_PART):
                            sp.dma_start(qscr[bs, s].rearrange("b p n -> p b n"),
                                         qparts[:, part, bs].rearrange("p b r t -> p b (r t)")).then_inc(q_stored[t], 16)
                        if t == 0:
                            sp.wait_ge(q_stored[0], 16 * SLOTS)
                            load_qstack(0, 0)
                if n == 0:
                    for t in range(1, TILES):
                        sp.wait_ge(q_stored[t], 16 * SLOTS)
                    sp.dma_start(swkv[:, :, 0:KV], swk_d.rearrange("(c p) n -> p c n", p=P)).then_inc(tail_weights_loaded, 16)
                    sp.dma_start(swkv[:, :, KV:2 * KV], swv_d.rearrange("(c p) n -> p c n", p=P)).then_inc(tail_weights_loaded, 16)
                    for g in range(G):
                        sp.dma_start(swo[HD * g:HD * g + HD],
                                     swo_d[R * HD * g:R * HD * (g + 1)].rearrange("(r d) n -> d r n", r=R)).then_inc(tail_weights_loaded, 16)

            slots(sp, slot, 1, between)
            for t in range(TILES):
                sp.wait_ge(out_ready, t + 1)
                sp.dma_start(of[t], xn[:, t]).then_inc(out_stored, 16)
            sp.wait_ge(out_stored, 16 * TILES)

        @block.gpsimd
        def _(pool):
            nc.gpsimd.memset(vaug[:, :, :, :, HD:VW], 1.0).then_inc(ones_ready, 1)

            nc.gpsimd.memset(zeros[:], 0.0).then_inc(zeros_ready, 1)
            pool.wait_ge(zeros_ready, 1)
            pool.wait_ge(xwq_loaded, 16)
            for c in range(C):
                nc.gpsimd.tensor_copy(wq_dg[:, c].rearrange("p r (d g) -> p r d g", g=G),
                                      xwq[:, c].rearrange("p (g r d) -> p r d g", g=G, r=R)).then_inc(wq_ordered, 1)

            def key_parts(m, trip):
                wait(pool, k_res, 1, m, 1, trip)
                wait_ring(pool, k_stored, m - 2, trip, SLOTS)
                nc.gpsimd.tensor_tensor(kparts[:, m % 2, 1], kres[:, m % 2], zeros[:], ALU.add).then_inc(k_mid, 1)
                wait(pool, k_mid, 1, m, 1, trip)
                nc.gpsimd.tensor_tensor(kparts[:, m % 2, 2], kres[:, m % 2], kparts[:, m % 2, 1], ALU.subtract).then_inc(k_low, 1)

            def max_parts(m, half, trip):
                nm = negmax[:, m % 2, HALF * half:HALF * half + HALF]
                wait(pool, max_ready, G, m, HALF * (half + 1), trip)
                wait(pool, m_transposed, 2, m - 1, half + 1, trip)
                nc.gpsimd.tensor_tensor(mparts[:, half, 0], nm, zeros[:, 0:HALF], ALU.add).then_inc(mpart_high, 1)
                wait(pool, mpart_high, 2, m, half + 1, trip)
                nc.gpsimd.tensor_tensor(maxres[:, half], nm, mparts[:, half, 0], ALU.subtract).then_inc(mpart_res, 1)
                wait(pool, mpart_res, 2, m, half + 1, trip)
                nc.gpsimd.tensor_tensor(mparts[:, half, 1], maxres[:, half], zeros[:, 0:HALF], ALU.add).then_inc(mpart_mid, 1)
                wait(pool, mpart_mid, 2, m, half + 1, trip)
                nc.gpsimd.tensor_tensor(mparts[:, half, 2], maxres[:, half], mparts[:, half, 1], ALU.subtract).then_inc(mpart_ready, 1)

            def slot(n, trip):
                if live(n - 1, trip):
                    max_parts(n - 1, 1, trip)
                if live(n + 1, trip):
                    key_parts(n + 1, trip)
                if live(n, trip):
                    max_parts(n, 0, trip)
                for g in range(G):
                    early(n, g, steps)

            def queries(t):
                pool.wait_ge(sq_turned, t + 1)
                nc.gpsimd.tensor_tensor(q_rot[:, t], q_rot[:, t], rotq_b[:, t % 2], ALU.add).then_inc(q_rot_ready, 1)

            def keys_values(t):
                if t == 0:
                    pool.wait_ge(k_low, B)
                    nc.gpsimd.tensor_copy(spread, ident[:].rearrange("p (b k) -> p b k", b=BPT).unsqueeze(2).to_broadcast([P, BPT, HALF, S])
                                          ).then_inc(spread_ready, 1)
                    pool.wait_ge(consts_loaded, 80)
                pool.wait_ge(sk_turned, t + 1)
                nc.gpsimd.tensor_tensor(k_rot[:, t], k_rot[:, t], rotk_b[:, t], ALU.add).then_inc(k_rot_ready, 1)

            def heads_to_columns(t):
                pool.wait_ge(k2T_ready, t + 1)
                nc.gpsimd.tensor_tensor(kbd[:, t], k2T[:, t].rearrange("p (b k) -> p b k", b=BPT).unsqueeze(2).to_broadcast([P, BPT, G, S]),
                                        group_mask[:].unsqueeze(1).unsqueeze(3).to_broadcast([P, BPT, G, S]), ALU.mult).then_inc(kbd_ready, 1)

            def probabilities(t):
                pool.wait_ge(rsum_ready, t + 1)
                nc.gpsimd.tensor_tensor(p2[:, t], p2[:, t], ssum[:, t].unsqueeze(3).to_broadcast([P, BPT, G, S]), ALU.mult).then_inc(p2_scaled, 1)

            def transpose2(t):
                pool.wait_ge(xn_ready[1], t + 1)
                nc.gpsimd.tensor_tensor(xs[:, t], xs[:, t], bias[:], ALU.add).then_inc(x2b_ready, 1)

            nothing = lambda t: None
            steps = {step: nothing for step in STEPS}
            steps.update(queries=queries, keys_values=keys_values, heads_to_columns=heads_to_columns,
                         probabilities=probabilities, transpose2=transpose2)

            def between(n):
                if n == -2:
                    for r in range(R):
                        res = xh[:, r].rearrange("p (b t) -> p b t", t=S)
                        pool.wait_ge(q_res, r + 1)
                        nc.gpsimd.tensor_copy(qparts[:, 1, :, r], res).then_inc(q_mid, 1)
                        pool.wait_ge(q_mid, r + 1)
                        nc.gpsimd.tensor_tensor(qparts[:, 2, :, r], res, qparts[:, 1, :, r], ALU.subtract).then_inc(q_low, 1)
                if n == -1:
                    wide = wnat.rearrange("p (n k) -> p n k", k=GS)
                    pool.wait_ge(packed_loaded, 32)
                    nc.gpsimd.tensor_scalar(wnorm[:, 1], wnorm[:, 0], 2.0, None, ALU.mult).then_inc(w_scaled, 1)
                    pool.wait_ge(w_scaled, 1)
                    pool.wait_ge(unpacked, 1)
                    nc.gpsimd.tensor_tensor(wide, wide, wnorm[:, 1].unsqueeze(2).to_broadcast([P, NGRP, GS]), ALU.mult).then_inc(w_step, 1)
                    pool.wait_ge(w_step, 1)
                    nc.gpsimd.tensor_tensor(wide, wide, wnorm[:, 0].unsqueeze(2).to_broadcast([P, NGRP, GS]), ALU.subtract).then_inc(w_ready, 1)

            slots(pool, slot, 2, between)

            late(steps)

        @block.scalar
        def _(act):
            act.dma_start(ident[:], ident_d).then_inc(ident_loaded, 16)
            act.dma_start(q3[:], q3_d.rearrange("(t p g) k -> p t (g k)", t=TILES, p=P)).then_inc(packed_loaded, 16)
            act.dma_start(wnorm[:, 0].rearrange("p (t g) -> p t g", t=TILES),
                          norm_d.rearrange("(t p g) a -> p t (g a)", t=TILES, p=P)).then_inc(packed_loaded, 16)
            act.dma_start(kstack[STACK:ROWS, 1].bitcast(I32), sel_d).then_inc(sel_loaded, 16)
            for dst, src in ((rope, rope_d), (causal.bitcast(I32), causal_d), (group_mask, group_mask_d), (batch_mask, batch_mask_d)):
                act.dma_start(dst[:], src).then_inc(consts_loaded, 16)
            act.dma_start(bias[:], bias_d.partition_broadcast(P)).then_inc(consts_loaded, 16)
            act.wait_ge(wkv_loaded, 32)
            nc.scalar.activation(wkv_h[:, 0].rearrange("p c (d g) -> p c d g", g=G),
                                 wkv_raw[:, 0].rearrange("p c (g d) -> p c d g", g=G), ACT.Copy).then_inc(wkv_high, 1)
            nc.scalar.activation(wkv_h[:, 1], wkv_raw[:, 1], ACT.Copy).then_inc(wkv_high, 1)
            act.wait_ge(ident_loaded, 16)
            nc.scalar.activation(ident_h[:], ident[:], ACT.Copy).then_inc(identh_ready, 1)

            def max_rows(m, half, trip):
                wait(act, m_transposed, 2, m, half + 1, trip)
                nc.scalar.activation(qstack[STACK:ROWS, m % 4, HALF * half:HALF * half + HALF],
                                     b_x[STACK:ROWS, 0:P // 2].bitcast(BF16).unsqueeze(1).to_broadcast([MROWS, HALF, P]),
                                     ACT.Copy).then_inc(mrows_ready, 1)

            def slot(n, trip):
                for g in range(G):
                    if g == 0 and live(n + 1, trip):
                        m = n + 1
                        wait(act, k_summed, 1, m, 1, trip)
                        wait_ring(act, k_stored, m - 2, trip, SLOTS)
                        nc.scalar.activation(kparts[:, m % 2, 0], b_k[:], ACT.Copy).then_inc(k_high, 1)
                    if g == 1 and live(n + 1, trip):
                        m = n + 1
                        wait(act, v_chunk, C, m, C, trip)
                        wait(act, v_transposed, 1, m, 0, trip)
                        nc.scalar.activation(vT[:], b_v[:], ACT.Copy).then_inc(vT_ready, 1)
                    if g % 2 == 0 and live(n + 2, trip):
                        m, c = n + 2, g // 2
                        wait(act, ctx_transposed, C, m, c + 1, trip)
                        wait(act, v_chunk, C, m - 1, c + 1, trip)
                        nc.scalar.activation(cT_h[:, c], b_t[:], ACT.Copy).then_inc(ctx_high, 1)
                    if live(n - 1, trip):
                        m = n - 1
                        wait(act, st_ready, G, m, g + 1, trip)
                        wait(act, pv_ready, 2, m - 1, g // HALF + 1, trip)
                        nc.scalar.activation(pT[:, g], b_c[g % 2][:].rearrange("p (a n) -> p a n", a=KT),
                                             ACT.Exp, scale=SCALE).then_inc(exp_ready, 1)
                    if g == 2 and live(n - 1, trip):
                        max_rows(n - 1, 1, trip)
                    if g == 2 and live(n - 2, trip):
                        m = n - 2
                        wait(act, pv_ready, 2, m, 2, trip)
                        wait(act, oraw_transposed, 1, m, 0, trip)
                        nc.scalar.activation(o_raw[:], b_d[:, 0:2 * P].rearrange("p (h n) -> p h n", h=2), ACT.Copy).then_inc(oraw_ready, 1)
                    if g == 7 and live(n, trip):
                        max_rows(n, 0, trip)
                    if n == B - 2 and g < C:
                        act.wait_ge(w_transposed, g + 1)
                        nc.scalar.activation(wT[:, g], b_y[:], ACT.Copy).then_inc(wT_ready, 1)
                    early(n, g, steps)

            def deviation(t, norm):
                act.wait_ge(ln_var[norm], t + 1)
                nc.scalar.activation(rstd[:, t:t + 1], mv[:, t, 1:2], ACT.Sqrt).then_inc(ln_std[norm], 1)

            def transposed(t, norm):
                act.wait_ge((xn_transposed, xn2_transposed)[norm], t + 1)
                nc.scalar.activation(xnT[:, t], (bank_y, bank_x)[norm][t][:].rearrange("p (c n) -> p c n", c=C),
                                     ACT.Copy).then_inc((xnT_ready, xnT2_ready)[norm], 1)

            def heads_to_columns(t):
                act.wait_ge(q_transposed, t + 1)
                nc.scalar.activation(q2T[:, t].rearrange("p b (r t) -> p r b t", r=R),
                                     bank_x[t][:].rearrange("p (r b t) -> p r b t", r=R, b=BPT), ACT.Copy).then_inc(q2T_ready, 1)
                act.wait_ge(k_transposed, t + 1)
                nc.scalar.activation(k2T[:, t], bank_y[t][:, 0:P], ACT.Copy).then_inc(k2T_ready, 1)

            def scores(t):
                for half in range(2):
                    act.wait_ge(ss_shifted, 2 * t + half + 1)
                    pair = p2[:, t, 2 * half:2 * half + 2]
                    nc.scalar.activation(pair, pair, ACT.Exp, scale=SCALE).then_inc(p2_ready, 1)

            def transpose_probabilities(t):
                for half in range(2):
                    act.wait_ge(p_transposed, 2 * t + half + 1)
                    nc.scalar.activation(pT2[:, t, 2 * half:2 * half + 2], (bank_x, bank_y)[half][t][:].rearrange("p (b h n) -> p b h n", b=2, h=2),
                                         ACT.Copy).then_inc(pT2_ready, 1)

            def attend(t):
                act.wait_ge(so_summed, t + 1)
                nc.scalar.activation(o2T[:, t].rearrange("p r b t -> p b r t"),
                                     bank_x[t][:].rearrange("p (b r t) -> p b r t", b=BPT, r=R), ACT.Copy).then_inc(o2T_ready, 1)

            nothing = lambda t: None
            steps = {step: nothing for step in STEPS}
            steps.update(residual1=lambda t: deviation(t, 0), transpose1=lambda t: transposed(t, 0), heads_to_columns=heads_to_columns,
                         scores=scores, transpose_probabilities=transpose_probabilities, attend=attend,
                         residual2=lambda t: deviation(t, 1), transpose2=lambda t: transposed(t, 1))

            def between(n):
                if n == -2:
                    act.wait_ge(ln1_var, 1)
                    nc.scalar.activation(rstd[:], mv[:, :, 1], ACT.Sqrt).then_inc(ln1_std, 1)
                    for t in range(TILES):
                        act.wait_ge(xh_transposed, t + 1)
                        nc.scalar.activation(xhT[:, :, P * t:P * t + P], (b_x, b_s)[t % 2][:].rearrange("p (c n) -> p c n", c=C),
                                             ACT.Copy).then_inc(xhT_ready, 1)
                    for r in range(R):
                        act.wait_ge(q_summed, r + 1)
                        nc.scalar.activation(qparts[:, 0, :, r], b_c[r % 2][:].rearrange("p (b t) -> p b t", t=S),
                                             ACT.Copy).then_inc(q_high, 1)
                    for g in range(G):
                        act.dma_start(wo[HD * g:HD * g + HD],
                                      xwo_d[R * HD * g:R * HD * (g + 1)].rearrange("(r d) n -> d r n", r=R)).then_inc(weights_loaded, 16)
                    act.dma_start(swq[:], swq_d.rearrange("(c p) n -> p c n", p=P)).then_inc(weights_loaded, 16)
                    act.wait_ge(unpacked, 1)
                    for i in (0, 2, 3):
                        act.dma_start(kstack[STACK:ROWS, i].bitcast(I32), sel_d).then_inc(sel_loaded, 16)

            slots(act, slot, 2, between)

            late(steps)

        @block.vector
        def _(dve):
            dve.wait_ge(wkv_high, 2)
            nc.vector.tensor_tensor(wkv_l[:, 0].rearrange("p c (d g) -> p c d g", g=G),
                                    wkv_raw[:, 0].rearrange("p c (g d) -> p c d g", g=G),
                                    wkv_h[:, 0].rearrange("p c (d g) -> p c d g", g=G).bitcast(F32), ALU.subtract).then_inc(wkv_split, 1)
            nc.vector.tensor_tensor(wkv_l[:, 1], wkv_raw[:, 1], wkv_h[:, 1].bitcast(F32), ALU.subtract).then_inc(wkv_split, 1)

            def normalise(m, trip):
                acc = b_d[:, 2 * P:].rearrange("p (g v) -> p g v", v=VW)
                wait(dve, oraw_transposed, 1, m, 1, trip)
                nc.vector.reciprocal(rden[:, m % 2], acc[:, :, HD]).then_inc(rden_ready, 1)
                wait(dve, rden_ready, 1, m, 1, trip)
                nc.vector.tensor_tensor(o_sb[:, m % 2], acc[:, :, 0:HD],
                                        rden[:, m % 2].unsqueeze(2).to_broadcast([P, G, HD]), ALU.mult).then_inc(o_ready, 1)

            def slot(n, trip):
                for g in range(G):
                    if live(n, trip):
                        wait(dve, s_ready, G, n, g + 1, trip)
                        if g % HALF == 0:
                            wait(dve, mpart_res, 2, n - 2, g // HALF + 1, trip)
                        nc.vector.tensor_reduce(negmax[:, n % 2, g:g + 1], b_s[:], AX, ALU.max, negate=True).then_inc(max_ready, 1)
                    if g == 0 and live(n + 1, trip):
                        m = n + 1
                        wait(dve, k_high, 1, m, 1, trip)
                        wait(dve, k_low, 1, m - 2, 1, trip)
                        nc.vector.tensor_tensor(kres[:, m % 2], b_k[:], kparts[:, m % 2, 0], ALU.subtract).then_inc(k_res, 1)
                    if g == 4 and live(n + 1, trip):
                        m = n + 1
                        wait(dve, v_transposed, 1, m, 1, trip)
                        nc.vector.tensor_copy(vaug[:, m % 4, :, :, 0:HD],
                                              b_x[:].rearrange("p (a g d) -> p a g d", a=KT, g=G)).then_inc(v_ready, 1)
                    if g % 2 == 0 and live(n + 2, trip):
                        m, c = n + 2, g // 2
                        wait(dve, ctx_high, C, m, c + 1, trip)
                        nc.vector.tensor_tensor(cT_l[:, c], b_t[:], cT_h[:, c].bitcast(F32), ALU.subtract).then_inc(ctx_low, 1)
                    if g == 3 and live(n - 2, trip):
                        normalise(n - 2, trip)
                    if g == 5 and live(n - 2, trip):
                        m = n - 2
                        wait(dve, o_transposed, 1, m, 1, trip)
                        tile = m // BPT + trip
                        nc.vector.tensor_copy(oT[:, tile, :, S * (m % BPT):S * (m % BPT) + S],
                                              b_x[:, 0:P].rearrange("p (r t) -> p r t", r=R)).then_inc(oT_ready, 1)
                    early(n, g, steps)

            def between(n):
                if n == -2:
                    dve.wait_ge(x_loaded, 16)
                    for t in range(TILES):
                        nc.vector.bn_stats(st[:, t], xs[:, t]).then_inc(ln1_step, 1)
                    for t in range(TILES):
                        dve.wait_ge(ln1_step, t + 1)
                        nc.vector.bn_aggr(mv[:, t], st[:, t]).then_inc(ln1_step, 1)
                    dve.wait_ge(ln1_step, 2 * TILES)
                    nc.vector.tensor_scalar(mv[:, :, 1], mv[:, :, 1], EPS, None, ALU.add).then_inc(ln1_var, 1)
                    dve.wait_ge(ln1_std, 1)
                    nc.vector.reciprocal(rstd[:], rstd[:]).then_inc(ln1_step, 1)
                    dve.wait_ge(ln1_step, 2 * TILES + 1)
                    for t in range(TILES):
                        nc.vector.tensor_scalar(xh[:, t], xs[:, t], mv[:, t, 0:1], rstd[:, t:t + 1], ALU.subtract,
                                                ALU.mult).then_inc(xh_ready, 1)
                    for r in range(R):
                        dve.wait_ge(q_high, r + 1)
                        nc.vector.tensor_tensor(xh[:, r].rearrange("p (b t) -> p b t", t=S),
                                                b_c[r % 2][:].rearrange("p (b t) -> p b t", t=S),
                                                qparts[:, 0, :, r], ALU.subtract).then_inc(q_res, 1)
                    SHR, SHL, AND, OR = ALU.logical_shift_right, ALU.logical_shift_left, ALU.bitwise_and, ALU.bitwise_or
                    b0, b1, b2 = (qbytes[:, :, k] for k in range(3))
                    dve.wait_ge(packed_loaded, 32)
                    nc.vector.tensor_copy(qbytes.rearrange("p n k -> p (n k)"),
                                          q3[:].rearrange("p t n -> p (t n)").bitcast(U8)).then_inc(unpack_step, 1)
                    dve.wait_ge(unpack_step, 1)
                    nc.vector.tensor_scalar(bits[:, 0], b0, 6, 3, SHR, AND).then_inc(unpack_step, 1)
                    nc.vector.tensor_scalar(bits[:, 1], b1, 1, 2, AND, SHL).then_inc(unpack_step, 1)
                    nc.vector.tensor_scalar(bits[:, 2], b1, 7, 1, SHR, AND).then_inc(unpack_step, 1)
                    nc.vector.tensor_scalar(bits[:, 3], b2, 3, 1, AND, SHL).then_inc(unpack_step, 1)
                    for k, byte, shift in ((0, b0, 0), (1, b0, 3), (3, b1, 1), (4, b1, 4), (6, b2, 2), (7, b2, 5)):
                        nc.vector.tensor_scalar(qvals[:, :, k], byte, shift, 7, SHR, AND).then_inc(unpack_step, 1)
                    dve.wait_ge(unpack_step, 5)
                    nc.vector.tensor_tensor(qvals[:, :, 2], bits[:, 0], bits[:, 1], OR).then_inc(unpack_step, 1)
                    nc.vector.tensor_tensor(qvals[:, :, 5], bits[:, 2], bits[:, 3], OR).then_inc(unpack_step, 1)
                    dve.wait_ge(unpack_step, 13)
                    nc.vector.tensor_scalar(wnat, qvals.rearrange("p n k -> p (n k)"), 1.0 / 7.0, None, ALU.mult).then_inc(unpacked, 1)

            def residual(t, norm):
                if t == 0 and norm == 0:
                    dve.wait_ge(w_transposed, C)
                    dve.wait_ge(consts_loaded, 80)
                dve.wait_ge((wo_summed, swo_summed)[norm], t + 1)
                nc.vector.tensor_tensor(xs[:, t], (bank_x, bank_y)[norm][t][:], xs[:, t], ALU.add).then_inc((x1_ready, x2_ready)[norm], 1)
                dve.wait_ge((x1_ready, x2_ready)[norm], t + 1)
                nc.vector.bn_stats(st[:, t], xs[:, t]).then_inc(ln_stats[norm], 1)
                dve.wait_ge(ln_stats[norm], t + 1)
                nc.vector.bn_aggr(mv[:, t], st[:, t]).then_inc(ln_aggr[norm], 1)
                dve.wait_ge(ln_aggr[norm], t + 1)
                nc.vector.tensor_scalar(mv[:, t, 1:2], mv[:, t, 1:2], EPS, None, ALU.add).then_inc(ln_var[norm], 1)

            def normalise_rows(t, norm):
                dve.wait_ge(ln_std[norm], t + 1)
                nc.vector.reciprocal(rstd[:, t:t + 1], rstd[:, t:t + 1]).then_inc(ln_rstd[norm], 1)
                dve.wait_ge(ln_rstd[norm], t + 1)
                nc.vector.tensor_scalar(xn[:, t], xs[:, t], mv[:, t, 0:1], rstd[:, t:t + 1], ALU.subtract, ALU.mult).then_inc(xn_ready[norm], 1)

            def turn(src, a, b, shape, cs, sn, done):
                nc.vector.tensor_tensor(a, src, cs.to_broadcast(shape + [HD]), ALU.mult)
                nc.vector.tensor_tensor(b[..., 0:HD // 2], src[..., HD // 2:HD], sn[..., 0:HD // 2].to_broadcast(shape + [HD // 2]), ALU.mult)
                nc.vector.tensor_tensor(b[..., HD // 2:HD], src[..., 0:HD // 2], sn[..., HD // 2:HD].to_broadcast(shape + [HD // 2]), ALU.mult).then_inc(done, 1)

            cos = rope[:, 0].unsqueeze(1)
            sin = rope[:, 1].unsqueeze(1)

            def queries(t):
                dve.wait_ge(sq_summed, t + 1)
                count(dve, q_rot_ready, t - 1)
                a, b = (v.rearrange("p (r g d) -> p r g d", r=R, g=G) for v in (q_rot[:, t], rotq_b[:, t % 2]))
                turn(bank_x[t][:].rearrange("p (g r d) -> p r g d", g=G, r=R), a, b, [P, R, G], cos.unsqueeze(1), sin.unsqueeze(1), sq_turned)

            def keys_values(t):
                dve.wait_ge(skv_summed, t + 1)
                src, a, b = (v.rearrange("p (g d) -> p g d", g=G) for v in (bank_y[t][:, 0:KV], k_rot[:, t], rotk_b[:, t]))
                turn(src, a, b, [P, G], cos, sin, sk_turned)
                nc.vector.tensor_copy(v2[:, t], bank_y[t][:, KV:2 * KV]).then_inc(v2_ready, 1)

            def spread_values(t):
                dve.wait_ge(v_spread, t + 1)
                nc.vector.tensor_tensor(vbd[:, t].rearrange("p b (h j d) -> p (b h) j d", h=2, j=HALF),
                                        bank_x[t][:].rearrange("p (x j d) -> p x j d", j=HALF, d=HD),
                                        batch_mask[:].unsqueeze(1).unsqueeze(3).to_broadcast([P, 2 * BPT, HALF, HD]), ALU.mult).then_inc(vbd_ready, 1)

            def scores(t):
                for half in range(2):
                    k = 2 * t + half
                    src = (bank_x, bank_y)[half][t][:].rearrange("p (b g k) -> p b g k", b=2, g=G)
                    top = smax[:, t, 2 * half:2 * half + 2]
                    dve.wait_ge(ss_summed, k + 1)
                    nc.vector.tensor_reduce(top, src, AX, ALU.max).then_inc(smax_ready, 1)
                    dve.wait_ge(smax_ready, k + 1)
                    nc.vector.tensor_tensor(p2[:, t, 2 * half:2 * half + 2], src, top.unsqueeze(3).to_broadcast([P, 2, G, S]), ALU.subtract).then_inc(ss_shifted, 1)

            def probabilities(t):
                dve.wait_ge(p2_ready, 2 * t + 2)
                nc.vector.tensor_reduce(ssum[:, t], p2[:, t], AX, ALU.add).then_inc(ssum_ready, 1)
                dve.wait_ge(ssum_ready, t + 1)
                nc.vector.reciprocal(ssum[:, t], ssum[:, t]).then_inc(rsum_ready, 1)

            def feed_forward(t):
                dve.wait_ge(x2b_ready, t + 1)
                dve.wait_ge(ffn_summed, t + 1)
                nc.vector.tensor_tensor(xn[:, t], bank_y[t][:], xs[:, t], ALU.add).then_inc(out_ready, 1)

            nothing = lambda t: None
            steps = {step: nothing for step in STEPS}
            steps.update(residual1=lambda t: residual(t, 0), normalise1=lambda t: normalise_rows(t, 0), queries=queries,
                         keys_values=keys_values, spread_values=spread_values, scores=scores, probabilities=probabilities,
                         residual2=lambda t: residual(t, 1), normalise2=lambda t: normalise_rows(t, 1), feed_forward=feed_forward)
            slots(dve, slot, 2, between)
            late(steps)

        @block.tensor
        def _(pe):
            def ctx_chunk(m, c, trip):
                if c == 0:
                    wait_ring(pe, ctx_loaded, m, trip)
                wait(pe, ctx_low, C, m, c, trip)
                for a in range(KT):
                    last = nc.tensor.transpose(b_t[:, P * a:P * a + P], cx[:, m % 2, a, P * c:P * c + P], ident[:])
                last.then_inc(ctx_transposed, 1)

            def project(m, which, c, trip):
                wait(pe, ctx_low, C, m, c + 1, trip)
                if c == 0:
                    wait(pe, vT_ready if which else k_res, 1, m, 0, trip)
                out = (b_k, b_v)[which][:]
                nc.tensor.matmul(out, wkv_h[:, which, c], cT_h[:, c], start=(c == 0), stop=False)
                nc.tensor.matmul(out, wkv_l[:, which, c], cT_h[:, c], start=False, stop=False)
                last = nc.tensor.matmul(out, wkv_h[:, which, c], cT_l[:, c], start=False, stop=(c == C - 1))
                if which == 1:
                    last.then_inc(v_chunk, 1)
                elif c == C - 1:
                    last.then_inc(k_summed, 1)

            def max_rows(m, half, trip):
                wait(pe, mpart_ready, 2, m, half + 1, trip)
                nc.tensor.transpose(b_x[STACK:ROWS, 0:P // 2].bitcast(BF16),
                                    mparts[:, half].rearrange("p k j -> p (k j)"), ident_h[:]).then_inc(m_transposed, 1)

            def times_v(m, half, trip):
                wait(pe, exp_ready, G, m, HALF * (half + 1), trip)
                if half == 0:
                    wait(pe, v_ready, 1, m, 1, trip)
                    wait(pe, o_ready, 1, m, 0, trip)
                for a in range(KT):
                    for j in range(HALF):
                        g = HALF * half + j
                        last = nc.tensor.matmul(b_d[VW * j:VW * j + VW, P * half:P * half + P], vaug[:, m % 4, a, g],
                                                pT[:, g, a], start=(a == 0), stop=(a == KT - 1))
                last.then_inc(pv_ready, 1)

            def slot(n, trip):
                for g in range(G):
                    if live(n, trip):
                        if g == 0:
                            wait_ring(pe, kstack_loaded, n, trip)
                            wait_ring(pe, qstack_loaded, n, trip)
                        wait(pe, max_ready, G, n, g, trip)
                        nc.tensor.matmul(b_s[:], qstack[0:STACK, n % 4, g], kstack[0:STACK, n % 4, g],
                                         start=True, stop=True).then_inc(s_ready, 1)
                    if g % 2 == 0 and live(n + 2, trip):
                        ctx_chunk(n + 2, g // 2, trip)
                    if live(n - 1, trip):
                        m = n - 1
                        wait(pe, exp_ready, G, m, g - 1, trip)
                        if g % HALF == 0:
                            wait(pe, mrows_ready, 2, m, g // HALF + 1, trip)
                        for a in range(KT):
                            last = nc.tensor.matmul(b_c[g % 2][:, P * a:P * a + P], kstack[0:ROWS, m % 4, g, P * a:P * a + P],
                                                    qstack[0:ROWS, m % 4, g], start=True, stop=True)
                        last.then_inc(st_ready, 1)
                    if g == 1 and live(n - 2, trip):
                        times_v(n - 2, 1, trip)
                    if g == 6 and live(n - 1, trip):
                        times_v(n - 1, 0, trip)
                    if g == 2 and live(n - 1, trip):
                        wait(pe, mrows_ready, 2, n - 1, 1, trip)
                        max_rows(n - 1, 1, trip)
                    if g == 3 and live(n + 1, trip):
                        m = n + 1
                        wait(pe, vT_ready, 1, m, 1, trip)
                        if live(n - 1, trip):
                            wait(pe, mrows_ready, 2, n - 1, 2, trip)
                        for a in range(KT):
                            last = nc.tensor.transpose(b_x[:, P * a:P * a + P], vT[:, P * a:P * a + P], ident[:])
                        last.then_inc(v_transposed, 1)
                    if g == 3 and live(n - 2, trip):
                        m = n - 2
                        wait(pe, oraw_ready, 1, m, 1, trip)
                        for half in range(2):
                            last = nc.tensor.transpose(b_d[:, P * (2 + half):P * (3 + half)], o_raw[:, half], ident[:])
                        last.then_inc(oraw_transposed, 1)
                    if g == 5 and live(n - 2, trip):
                        m = n - 2
                        if live(n + 1, trip):
                            wait(pe, v_ready, 1, n + 1, 1, trip)
                        elif live(n - 1, trip):
                            wait(pe, mrows_ready, 2, n - 1, 2, trip)
                        wait(pe, o_ready, 1, m, 1, trip)
                        nc.tensor.transpose(b_x[:, 0:P], o_sb[:, m % 2].rearrange("p g d -> p (g d)"), ident[:]).then_inc(o_transposed, 1)
                    if g == 6 and live(n, trip):
                        if live(n + 1, trip):
                            wait(pe, v_ready, 1, n + 1, 1, trip)
                        if live(n - 2, trip):
                            wait(pe, oT_ready, 1, n - 2, 1, trip)
                        if not looped(trip) and n == 0:
                            pe.wait_ge(identh_ready, 1)
                            pe.wait_ge(sel_loaded, 64)
                        max_rows(n, 0, trip)
                    if n == B - 2 and g < C:
                        pe.wait_ge(w_ready, 1)
                        pe.wait_ge(ctx_low, C * B)
                        count(pe, wT_ready, g)
                        for t in range(TILES):
                            at = D * t + P * g
                            last = nc.tensor.transpose(b_y[:, P * t:P * t + P], wnat[:, at:at + P], ident[:])
                        last.then_inc(w_transposed, 1)
                    if not looped(trip) and n == -2 and g == 1:
                        pe.wait_ge(wkv_split, 2)
                    if g % 2 and live(n + 2, trip):
                        project(n + 2, 0, g // 2, trip)
                    if g == 0 and live(n + 1, trip):
                        project(n + 1, 1, C - 1, trip)
                    if g in (2, 4, 6) and live(n + 2, trip):
                        project(n + 2, 1, g // 2 - 1, trip)
                    early(n, g, steps)

            def rows_by(lhsT, weight, chunks, out, done):
                for c in range(chunks):
                    last = nc.tensor.matmul(out, lhsT(c), weight(c), start=(c == 0), stop=(c == chunks - 1))
                last.then_inc(done, 1)

            def residual1(t):
                pe.wait_ge(oT_ready, BPT * (t + 1))
                if t == 0:
                    pe.wait_ge(weights_loaded, 16 * (G + 1))
                    pe.wait_ge(tail_weights_loaded, 16 * (G + 2))
                for semaphore, value in (((k_res, B), (vT_ready, B)), ((wT_ready, C), (max_ready, G * B)), ((exp_ready, G * B),), ())[t]:
                    pe.wait_ge(semaphore, value)
                rows_by(lambda r: oT[:, t, r], lambda r: wo[:, r], R, bank_x[t][:], wo_summed)

            def transpose_rows(t, norm):
                pe.wait_ge(xn_ready[norm], t + 1)
                for c in range(C):
                    last = nc.tensor.transpose((bank_y, bank_x)[norm][t][:, P * c:P * c + P], xn[:, t, P * c:P * c + P], ident[:])
                last.then_inc((xn_transposed, xn2_transposed)[norm], 1)

            def queries(t):
                pe.wait_ge(xnT_ready, t + 1)
                rows_by(lambda c: xnT[:, t, c], lambda c: swq[:, c], C, bank_x[t][:], sq_summed)

            def keys_values(t):
                pe.wait_ge(xnT_ready, t + 1)
                rows_by(lambda c: xnT[:, t, c], lambda c: swkv[:, c], C, bank_y[t][:, 0:2 * KV], skv_summed)

            def heads_to_columns(t):
                pe.wait_ge(q_rot_ready, t + 1)
                for r in range(R):
                    last = nc.tensor.transpose(bank_x[t][:, P * r:P * r + P], q_rot[:, t, P * r:P * r + P], ident[:])
                last.then_inc(q_transposed, 1)
                pe.wait_ge(k_rot_ready, t + 1)
                pe.wait_ge(v2_ready, t + 1)
                nc.tensor.transpose(bank_y[t][:, 0:P], k_rot[:, t], ident[:]).then_inc(k_transposed, 1)

            def spread_values(t):
                pe.wait_ge(q2T_ready, t + 1)
                pe.wait_ge(spread_ready, 1)
                for b in range(BPT):
                    last = nc.tensor.matmul(bank_x[t][:, P * b:P * b + P], spread[:, b].rearrange("p j k -> p (j k)"), v2[:, t],
                                            start=True, stop=True)
                last.then_inc(v_spread, 1)

            def scores(t):
                pe.wait_ge(kbd_ready, t + 1)
                pe.wait_ge(vbd_ready, t + 1)
                for half in range(2):
                    out = (bank_x, bank_y)[half][t]
                    nc.tensor.matmul(out[:], ident_h[:], causal[:], start=True, stop=False)
                    for i in range(2):
                        last = nc.tensor.matmul(out[:, G * S * i:G * S * (i + 1)], q2T[:, t, 2 * half + i],
                                                kbd[:, t, 2 * half + i].rearrange("p g k -> p (g k)"), start=False, stop=(i == 1))
                    last.then_inc(ss_summed, 1)

            def transpose_probabilities(t):
                pe.wait_ge(p2_scaled, t + 1)
                for half in range(2):
                    for x in range(4):
                        b, h = 2 * half + x // 2, x % 2
                        last = nc.tensor.transpose((bank_x, bank_y)[half][t][:, P * x:P * x + P],
                                                   p2[:, t, b, HALF * h:HALF * h + HALF].rearrange("p g k -> p (g k)"), ident[:])
                    last.then_inc(p_transposed, 1)

            def attend(t):
                pe.wait_ge(pT2_ready, 2 * t + 2)
                for b in range(BPT):
                    for h in range(2):
                        last = nc.tensor.matmul(bank_x[t][KV // 2 * h:KV // 2 * (h + 1), P * b:P * b + P],
                                                vbd[:, t, b, KV // 2 * h:KV // 2 * (h + 1)], pT2[:, t, b, h], start=True, stop=True)
                last.then_inc(so_summed, 1)

            def residual2(t):
                pe.wait_ge(o2T_ready, t + 1)
                rows_by(lambda r: o2T[:, t, r].rearrange("p b t -> p (b t)"), lambda r: swo[:, r], R, bank_y[t][:], swo_summed)

            def feed_forward(t):
                pe.wait_ge(xnT2_ready, t + 1)
                pe.wait_ge(wT_ready, C)
                rows_by(lambda c: xnT[:, t, c], lambda c: wT[:, c], C, bank_y[t][:], ffn_summed)

            nothing = lambda t: None
            steps = {step: nothing for step in STEPS}
            steps.update(residual1=residual1, transpose1=lambda t: transpose_rows(t, 0), queries=queries, keys_values=keys_values,
                         heads_to_columns=heads_to_columns, spread_values=spread_values, scores=scores,
                         transpose_probabilities=transpose_probabilities, attend=attend, residual2=residual2,
                         transpose2=lambda t: transpose_rows(t, 1), feed_forward=feed_forward)

            def between(n):
                if n == -2:
                    for t in range(TILES):
                        pe.wait_ge(xh_ready, t + 1)
                        count(pe, xhT_ready, t - 1)
                        for c in range(C):
                            last = nc.tensor.transpose((b_x, b_s)[t % 2][:, P * c:P * c + P], xh[:, t, P * c:P * c + P], ident[:])
                        last.then_inc(xh_transposed, 1)
                    pe.wait_ge(xhT_ready, TILES)
                    pe.wait_ge(wq_ordered, C)
                    for r in range(R):
                        count(pe, q_res, r - 1)
                        for c in range(C):
                            last = nc.tensor.matmul(b_c[r % 2][:], wq_dg[:, c, r], xhT[:, c], start=(c == 0), stop=(c == C - 1))
                        last.then_inc(q_summed, 1)
                    pe.wait_ge(q_res, R)

            pe.wait_ge(ident_loaded, 16)
            slots(pe, slot, 2, between)

            late(steps)


_INS = ["x", "ctx_4096", "L0_xattn_Wq", "L0_xattn_Wk", "L0_xattn_Wv", "L0_xattn_Wo", "L0_attn_Wq", "L0_attn_Wk",
        "L0_attn_Wv", "L0_attn_Wo", "L0_ffn_weight_q3", "L0_ffn_weight_norm", "L0_ffn_bias"]


def kernel(**inputs):
    import numpy as _np
    import concourse.bacc as _bacc
    from concourse import mybir as _mybir
    from concourse.bass_utils import run_bass_kernel_spmd as _run

    nc = _bacc.Bacc("TRN2", target_bir_lowering=False, num_devices=1)
    arrays = {name: _np.ascontiguousarray(inputs[name]) for name in _INS}
    arrays["L0_ffn_weight_q3"] = arrays["L0_ffn_weight_q3"].view(_np.int32)
    arrays.update(constants())
    args = []
    feeds = {}
    for name, a in arrays.items():
        feeds[f"in_{name}_dram"] = a
        args.append(nc.dram_tensor(f"in_{name}_dram", a.shape, _mybir.dt.from_np(a.dtype), kind="ExternalInput").ap())
    out = nc.dram_tensor("out_dram", (B, S, D), F32, kind="ExternalOutput").ap()
    perceiver(nc, *args, out)
    r = _run(nc, [feeds], core_ids=[0])
    return r.results[0]["out_dram"]
```

```python
from contextlib import ExitStack

import numpy as np

import concourse.bass as bass
from concourse import mybir
from concourse.alu_op_type import AluOpType as ALU

F32 = mybir.dt.float32
F32R = mybir.dt.float32r
BF16 = mybir.dt.bfloat16
I32 = mybir.dt.int32
U8 = mybir.dt.uint8
ACT = mybir.ActivationFunctionType
AX = mybir.AxisListType.X

P = 128
B, S, D, KEYS = 16, 32, 512, 512
HEADS, G, HD = 32, 8, 16
R = HEADS // G
KV = G * HD
C = D // P
KT = KEYS // P
TOK = B * S
TILES = TOK // P
BPT = P // S
GS = 32
SCALE = float(HD) ** -0.5
EPS = 1e-5
MASKED = -1e30
NGRP = D * TILES // GS
NTRIP = NGRP * GS // 8

CHUNKED = ("residual1", "queries", "keys_values")
STEPS = [(step, c) for step in ("residual1", "normalise1", "transpose1", "queries", "keys_values", "heads_to_columns",
                                "spread_values", "scores", "probabilities", "transpose_probabilities", "attend",
                                "residual2", "normalise2", "transpose2", "feed_forward")
         for c in range(C if step in CHUNKED else 1)]
SPLIT_AT = {(14, 1): 0, (14, 2): 1, (14, 4): 2, (14, 5): 3, (14, 6): 4, (14, 7): 5}
EARLY = {(14, 3): [(0, 0)], (14, 5): [(1, 0)], (14, 7): [(2, 0)], (15, 0): [(3, 0), (4, 0)],
         (15, 1): [(5, 0), (0, 1)], (15, 2): [(1, 1), (6, 0), (7, 0)], (15, 3): [(2, 1)], (15, 4): [(8, 0), (3, 1)],
         (15, 5): [(9, 0), (10, 0), (11, 0), (12, 0)], (15, 7): [(4, 1)], (16, 0): [(13, 0), (5, 1)],
         (16, 2): [(6, 1), (7, 1)], (16, 3): [(8, 1)], (16, 5): [(9, 1), (10, 1), (11, 1)],
         (16, 7): [(12, 1), (13, 1)], (17, 1): [(0, 2), (1, 2)], (17, 2): [(2, 2), (3, 2), (14, 0)],
         (17, 4): [(4, 2), (14, 1)], (17, 7): [(5, 2)]}
LATE = [(0, 3), (1, 3), (2, 3), (3, 3), (6, 2), (7, 2), (8, 2), (4, 3), (9, 2), (10, 2), (5, 3), (11, 2), (12, 2),
        (15, 0), (6, 3), (13, 2), (16, 0), (7, 3), (8, 3), (9, 3), (10, 3), (11, 3), (14, 2), (12, 3), (13, 3),
        (15, 1), (17, 0), (16, 1), (14, 3), (15, 2), (17, 1), (18, 0), (16, 2), (15, 3), (19, 0), (18, 1), (17, 2),
        (20, 0), (19, 1), (16, 3), (17, 3), (18, 2), (20, 1), (21, 0), (19, 2), (18, 3), (21, 1), (22, 0), (20, 2),
        (19, 3), (22, 1), (23, 0), (21, 2), (20, 3), (21, 3), (22, 2), (23, 1), (22, 3), (23, 2), (23, 3)]

K_PART = (0, 0, 0, 1, 1, 2)
Q_PART = (0, 1, 2, 0, 1, 0)
SLOTS = len(K_PART)
STACK = SLOTS * HD
HALF = G // 2
MROWS = 3 * HALF
ROWS = STACK + MROWS
VW = HD + 1
TILE = 32


def constants():
    inv = (1.0 / np.float32(10000.0) ** (np.arange(0, HD, 2, dtype=np.float32)[: HD // 2] / np.float32(HD))).astype(np.float32)
    ang = np.arange(S, dtype=np.float32)[:, None] * inv[None, :]
    cos, sin = np.cos(ang).astype(np.float32), np.sin(ang).astype(np.float32)
    rope = np.stack([np.concatenate([cos, cos], 1), np.concatenate([-sin, sin], 1)], 1)
    rope = np.tile(rope, (P // S, 1, 1)).astype(np.float32)
    t = np.arange(P) % S
    causal = np.where(np.arange(2 * G * S)[None, :] % S <= t[:, None], 0.0, MASKED).astype(np.float32)
    causal = np.ascontiguousarray((causal.view(np.uint32) >> 16).astype(np.uint16)).view(np.int32)
    group_of_row = (np.arange(P)[:, None] // HD == np.arange(G)[None, :]).astype(np.float32)
    batch_of_row = (np.arange(P)[:, None] // S == np.arange(BPT)[None, :]).astype(np.float32)
    pair = 0x3F803F80
    sel = np.zeros((MROWS, G, KEYS // 2), np.int32)
    for row in range(MROWS):
        sel[row, np.arange(G) % HALF == row % HALF] = pair
    return {"rope": rope, "causal": causal, "group_mask": group_of_row, "batch_mask": batch_of_row,
            "sel": sel, "ident": np.eye(P, dtype=np.float32)}


def perceiver(nc, x_d, ctx_d, xwq_d, xwk_d, xwv_d, xwo_d, swq_d, swk_d, swv_d, swo_d, q3_d, norm_d, bias_d,
              rope_d, causal_d, group_mask_d, batch_mask_d, sel_d, ident_d, out_d):
    kscr = nc.dram_tensor("kscr", [2, SLOTS, KV, KEYS], BF16).ap()
    qscr = nc.dram_tensor("qscr", [TILES, SLOTS, KV, BPT, P], BF16).ap()
    xf = x_d.rearrange("b s d -> (b s) d").rearrange("(t p) d -> p t d", p=P)
    of = out_d.rearrange("b s d -> (b s) d").rearrange("(t p) d -> t p d", p=P)

    with ExitStack() as ctx:
        def sb(name, shape, dt=F32):
            return ctx.enter_context(nc.sbuf_tensor(name, shape, dt))

        def sem(name):
            return ctx.enter_context(nc.semaphore(name))

        ident = sb("ident_sb", [P, P])
        ident_h = sb("ident_h", [P, P], BF16)
        rope = sb("rope_sb", [P, 2, HD])
        causal = sb("causal_sb", [P, 2 * G * S], BF16)
        group_mask = sb("group_mask_sb", [P, G])
        batch_mask = sb("batch_mask_sb", [P, BPT])
        bias = sb("bias_sb", [P, D])
        wkv_raw = sb("wkv_raw", [P, 2, C, KV])
        wkv_h = sb("wkv_h", [P, 2, C, KV], F32R)
        wkv_l = sb("wkv_l", [P, 2, C, KV], F32R)
        swq_h, swq_l, wT_h, wT_l = (sb(name, [P, C, D], F32R) for name in ("swq_h", "swq_l", "wT_h", "wT_l"))
        cx = sb("cx", [P, 2, KT, D])
        cT_h = sb("cT_h", [P, C, KEYS], F32R)
        cT_l = sb("cT_l", [P, C, KEYS], F32R)
        kparts = sb("kparts", [P, 2, 3, KEYS], BF16)
        kres = sb("kres", [P, KEYS])
        vT = sb("vT", [P, KEYS])
        vaug = sb("vaug", [P, 4, KT, G, VW])
        kstack = sb("kstack", [P, 4, G, KEYS], BF16)
        qstack = sb("qstack", [P, 4, G, P], BF16)
        zeros = sb("zeros", [P, KEYS], BF16)
        negmax = sb("negmax", [P, 2, G])
        maxres = sb("maxres", [P, 2, HALF])
        mparts = sb("mparts", [P, 2, 3, HALF], BF16)
        rden = sb("rden", [P, 2, G])
        o_raw = sb("o_raw", [P, 2, P])
        o_sb = sb("o_sb", [P, 2, G, HD])
        oT = sb("oT", [P, TILES, R, P])
        xs = sb("xs", [P, TILES, D])
        st = sb("st", [P, TILES, 6])
        mv = sb("mv", [P, TILES, 2])
        rstd = sb("rstd", [P, TILES])
        q3 = sb("q3_sb", [P, TILES, D // GS * 3], I32)
        wnorm = sb("wnorm", [P, 2, NGRP])

        region = sb("region", [P, 11264])

        def carve(sizes):
            at, parts = 0, []
            for size in sizes:
                parts.append(region[:, at:at + size])
                at += size
            assert at <= 11264
            return parts

        xwq, xhT, xh, qparts, wnat = carve((2048, 2048, 2048, 3072, 2048))
        pT = region[:, 0:G * KT * P].rearrange("p (g a n) -> p g a n", g=G, a=KT)
        xwq = xwq.rearrange("p (c n) -> p c n", c=C)
        xhT = xhT.rearrange("p (c n) -> p c n", c=C)
        xh = xh.rearrange("p (t n) -> p t n", t=TILES)
        qparts = qparts.bitcast(BF16).rearrange("p (k b r t) -> p k b r t", k=3, b=B, r=R)
        swkv, swo = region[:, 4096:5120], region[:, 5120:7168]
        swkv = swkv.rearrange("p (i c n) -> p i c n", i=2, c=C)
        swo = swo.rearrange("p (r n) -> p r n", r=R)
        by_tile = lambda words: words.rearrange("p (t n) -> p t n", t=TILES)
        xn = by_tile(region[:, 7168:9216])
        rotq_b = region[:, 9216:10240].rearrange("p (i n) -> p i n", i=2)
        k_rot = by_tile(region[:, 10240:10752])
        v2 = by_tile(region[:, 10752:11264])
        old_cx = cx[:].rearrange("p i a d -> p (i a d)")
        old_raw = wkv_raw[:].rearrange("p i c n -> p (i c n)")
        old_kstack = kstack[:].rearrange("p i g n -> p (i g n)").bitcast(F32)
        xnT_h, xnT_l = cT_h, cT_l
        wo = old_cx[:, 0:2048].rearrange("p (r n) -> p r n", r=R)
        swq = old_cx[:, 2048:4096].rearrange("p (c n) -> p c n", c=C)
        q_rot = by_tile(old_cx[:, 2048:4096])
        o2T = q_rot.rearrange("p t (r b n) -> p t r b n", r=R, b=BPT)
        rotk_b = by_tile(old_raw[:, 0:512])
        k2T = by_tile(old_raw[:, 512:1024])
        kbd = by_tile(region[:, 0:4096]).rearrange("p t (b g k) -> p t b g k", b=BPT, g=G)
        p2 = by_tile(old_kstack[:, 0:4096]).rearrange("p t (b g k) -> p t b g k", b=BPT, g=G)
        pT2 = by_tile(old_kstack[:, 4096:8192]).rearrange("p t (b h n) -> p t b h n", b=BPT, h=2)
        vbd = by_tile(vaug[:].rearrange("p i a g d -> p (i a g d)")[:, 0:2048]).rearrange("p t (b n) -> p t b n", b=BPT)
        q2T = by_tile(qstack[:].rearrange("p i g n -> p (i g n)").bitcast(F32)).rearrange("p t (b n) -> p t b n", b=BPT)
        spread = kres[:].rearrange("p (b j k) -> p b j k", b=BPT, j=HALF)
        smax = sb("smax", [P, TILES, BPT, G])
        ssum = sb("ssum", [P, TILES, BPT, G])

        scratch = kstack[:, 2:4].rearrange("p a g n -> p (a g n)").bitcast(F32)
        qbytes = scratch[:, 0:3 * NTRIP].bitcast(I32).rearrange("p (n k) -> p n k", k=3)
        qvals = scratch[:, 3 * NTRIP:11 * NTRIP].bitcast(I32).rearrange("p (n k) -> p n k", k=8)
        wq_dg = qstack[:].rearrange("p i g n -> p (i g n)").bitcast(F32).rearrange("p (c r n) -> p c r n", c=C, r=R)
        bits = scratch[:, 11 * NTRIP:15 * NTRIP].bitcast(I32).rearrange("p (k n) -> p k n", k=4)

        def bank(name):
            return ctx.enter_context(nc.psum_tensor(name, [P, 512], F32))

        b_t = bank("b_t")
        b_x = bank("b_x")
        b_k = bank("b_k")
        b_v = bank("b_v")
        b_s = bank("b_s")
        b_c = [bank(f"b_c{i}") for i in range(2)]
        b_d = bank("b_d")
        b_y = (b_t, b_s)
        bank_x, bank_y = (b_k, b_t, b_c[0], b_x), (b_v, b_s, b_c[1], b_d)

        names = """wkv_loaded consts_loaded ident_loaded x_loaded xwq_loaded sel_loaded packed_loaded
            wkv_high wkv_split identh_ready ones_ready ctx_transposed ctx_high ctx_low k_summed v_chunk k_high k_res
            k_mid k_low vT_ready v_transposed v_ready s_ready max_ready mpart_high mpart_res mpart_mid mpart_ready
            m_transposed mrows_ready st_ready exp_ready pv_ready oraw_ready oraw_transposed rden_ready o_ready o_transposed oT_ready
            ln1_step ln1_var ln1_std xh_ready xh_transposed xhT_ready q_summed q_high q_res q_mid q_low
            wq_ordered zeros_ready unpack_step unpacked w_scaled w_step w_ready w_transposed wT_high wT_ready swq_high swq_ready swkv_high swkv_ready pv_zero weights_loaded swkv_loaded swq_loaded tail_weights_loaded
            wo_summed x1_ready xn_transposed xnT_high xnT_ready
            sq_summed sq_turned q_rot_ready skv_summed sk_turned v2_ready k_rot_ready q_transposed q2T_ready spread_ready
            v_spread vbd_ready k_transposed k2T_ready kbd_ready ss_summed smax_ready ss_shifted p2_ready ssum_ready rsum_ready
            p2_scaled p_transposed pT2_ready so_summed o2T_ready swo_summed x2_ready xn2_transposed xnT2_high xnT2_ready x2b_ready
            ffn_summed out_ready out_stored"""
        sems = {name: sem(name) for name in names.split()}
        (wkv_loaded, consts_loaded, ident_loaded, x_loaded, xwq_loaded, sel_loaded, packed_loaded,
         wkv_high, wkv_split, identh_ready, ones_ready, ctx_transposed, ctx_high, ctx_low, k_summed, v_chunk, k_high, k_res,
         k_mid, k_low, vT_ready, v_transposed, v_ready, s_ready, max_ready, mpart_high, mpart_res, mpart_mid, mpart_ready,
         m_transposed, mrows_ready, st_ready, exp_ready, pv_ready, oraw_ready, oraw_transposed, rden_ready, o_ready, o_transposed, oT_ready,
         ln1_step, ln1_var, ln1_std, xh_ready, xh_transposed, xhT_ready, q_summed, q_high, q_res, q_mid, q_low,
         wq_ordered, zeros_ready, unpack_step, unpacked, w_scaled, w_step, w_ready, w_transposed, wT_high, wT_ready, swq_high, swq_ready, swkv_high, swkv_ready, pv_zero, weights_loaded, swkv_loaded, swq_loaded, tail_weights_loaded,
         wo_summed, x1_ready, xn_transposed, xnT_high, xnT_ready,
         sq_summed, sq_turned, q_rot_ready, skv_summed, sk_turned, v2_ready, k_rot_ready, q_transposed, q2T_ready, spread_ready,
         v_spread, vbd_ready, k_transposed, k2T_ready, kbd_ready, ss_summed, smax_ready, ss_shifted, p2_ready, ssum_ready, rsum_ready,
         p2_scaled, p_transposed, pT2_ready, so_summed, o2T_ready, swo_summed, x2_ready, xn2_transposed, xnT2_high, xnT2_ready, x2b_ready,
         ffn_summed, out_ready, out_stored) = (sems[name] for name in names.split())
        ln_stats, ln_aggr, ln_var, ln_std, ln_rstd, xn_ready = (
            [sem(f"{name}{i + 1}") for i in range(2)] for name in ("ln_stats", "ln_aggr", "ln_var", "ln_std", "ln_rstd", "xn_ready"))
        ctx_loaded = [sem(f"ctx_loaded{i}") for i in range(2)]
        k_stored = [sem(f"k_stored{i}") for i in range(2)]
        kstack_loaded = [sem(f"kstack_loaded{i}") for i in range(4)]
        qstack_loaded = [sem(f"qstack_loaded{i}") for i in range(4)]
        q_stored = [sem(f"q_stored{t}") for t in range(TILES)]

        FIRST, LAST, TRIPS = -2, B + 1, 3

        def slots(eng, slot, start, after=None):
            for n in range(FIRST, start):
                slot(n, 0)
                if after is not None:
                    after(n)
            with eng.Fori(0, TRIPS) as trip:
                for n in range(start, start + 4):
                    slot(n, trip)
            for n in range(start + 4 * TRIPS, LAST + 1):
                slot(n, 0)

        def looped(trip):
            return not isinstance(trip, int)

        def live(m, trip):
            return looped(trip) or 0 <= m < B

        def wait(eng, semaphore, per, m, extra, trip):
            base = per * m + extra
            if looped(trip):
                assert base >= 0
                eng.wait_ge(semaphore, 4 * per * trip + base)
            elif base > 0:
                eng.wait_ge(semaphore, base)

        def wait_ring(eng, semaphores, m, trip, dmas=1):
            ring = len(semaphores)
            base = 16 * dmas * (m // ring + 1)
            if looped(trip):
                eng.wait_ge(semaphores[m % ring], 16 * dmas * (4 // ring) * trip + base)
            elif m >= 0:
                eng.wait_ge(semaphores[m % ring], base)

        def splits_keys(n, g, trip):
            if not looped(trip) and (n, g) in ((-1, 7), (0, 0)):
                return g == 7
            return g == 0 and live(n + 1, trip)

        def count(eng, semaphore, value):
            if value > 0:
                eng.wait_ge(semaphore, value)

        def take(number, t, steps):
            step, c = STEPS[number]
            if step not in CHUNKED:
                steps[step](t)
            elif (step, "chunks") in steps:
                steps[step, "chunks"](t, c)
            elif c == C - 1:
                steps[step](t)

        def early(n, g, steps):
            for number, t in EARLY.get((n, g), ()):
                take(number, t, steps)

        def late(steps):
            for number, t in LATE:
                take(number, t, steps)

        block = ctx.enter_context(nc.Block())

        @block.sync
        def _(sp):
            def load_ctx(m, trip):
                sp.dma_start(cx[:, m % 2], ctx_d[4 * trip + m].rearrange("(p a) d -> p a d", a=KT)).then_inc(ctx_loaded[m % 2], 16)

            def load_qstack(m, trip):
                sp.dma_start(qstack[0:STACK, m % 4],
                             qscr[m // BPT + trip, :, :, m % BPT].rearrange("s (d g) n -> (s d) g n", g=G)).then_inc(qstack_loaded[m % 4], 16)

            for i, w in enumerate((xwk_d, xwv_d)):
                sp.dma_start(wkv_raw[:, i], w.rearrange("(c p) m -> p c m", p=P)).then_inc(wkv_loaded, 16)
            sp.dma_start(cx[:, 0], ctx_d[0].rearrange("(p a) d -> p a d", a=KT)).then_inc(ctx_loaded[0], 16)
            sp.dma_start(xs[:], xf).then_inc(x_loaded, 16)
            sp.dma_start(xwq, xwq_d.rearrange("(c p) n -> p c n", p=P)).then_inc(xwq_loaded, 16)
            sp.dma_start(cx[:, 1], ctx_d[1].rearrange("(p a) d -> p a d", a=KT)).then_inc(ctx_loaded[1], 16)
            sp.dma_start(kstack[STACK:ROWS, 1].bitcast(I32), sel_d).then_inc(sel_loaded, 16)
            sp.dma_start(q3[:], q3_d.rearrange("(t p g) k -> p t (g k)", t=TILES, p=P)).then_inc(packed_loaded, 16)
            sp.dma_start(wnorm[:, 0].rearrange("p (t g) -> p t g", t=TILES),
                          norm_d.rearrange("(t p g) a -> p t (g a)", t=TILES, p=P)).then_inc(packed_loaded, 16)
            for dst, src in ((rope, rope_d), (causal.bitcast(I32), causal_d), (group_mask, group_mask_d), (batch_mask, batch_mask_d)):
                sp.dma_start(dst[:], src).then_inc(consts_loaded, 16)
            sp.dma_start(bias[:], bias_d.partition_broadcast(P)).then_inc(consts_loaded, 16)

            def slot(n, trip):
                if not looped(trip):
                    load_weights(n)
                m = n + 1
                if looped(trip):
                    through, transposed, split, stored = (
                        sp.snap(step * trip + base) for step, base in
                        ((4 * G, max(1, G * (n - 2))), (4 * C, C * m + C), (4, m + 1), (32 * SLOTS, 16 * SLOTS * (m // 2 + 1))))
                else:
                    through, transposed, split, stored = max(1, G * (n - 2)), C * m + C, m + 1, 16 * SLOTS * (m // 2 + 1)
                if live(m, trip):
                    if looped(trip) or n >= 1:
                        sp.wait_ge(st_ready, through)
                    for part, done in enumerate((k_high, k_mid, k_low)):
                        sp.wait_ge(done, split)
                        for s in range(SLOTS):
                            if s == 1 and part == 0 and live(n + 3, trip):
                                sp.wait_ge(ctx_transposed, transposed)
                            if K_PART[s] == part:
                                sp.dma_start(kscr[m % 2, s], kparts[:, m % 2, part]).then_inc(k_stored[m % 2], 16)
                        if part == 0 and not looped(trip) and n == 0:
                            sp.wait_ge(q_stored[0], 16 * SLOTS)
                            load_qstack(0, 0)
                        if part == 2 and live(n + 3, trip) and (looped(trip) or n != 0):
                            load_ctx(n + 3, trip)
                if not looped(trip) and n == 0:
                    load_ctx(3, 0)
                if live(m, trip):
                    sp.wait_ge(k_stored[m % 2], stored)
                    if not looped(trip) and m in (2, 3):
                        sp.wait_ge(unpacked, 1)
                    sp.dma_start(kstack[0:STACK, m % 4],
                                 kscr[m % 2].rearrange("s (d g) n -> (s d) g n", g=G)).then_inc(kstack_loaded[m % 4], 16)
                    if looped(trip) or m > 0:
                        load_qstack(m, trip)

            def store_queries(t):
                for part, done in enumerate((q_high, q_mid, q_low)):
                    sp.wait_ge(done, R)
                    for s in range(SLOTS):
                        if Q_PART[s] == part:
                            sp.dma_start(qscr[t, s].rearrange("p b n -> p (b n)"),
                                         qparts[:, part, BPT * t:BPT * t + BPT].rearrange("p b r t -> p (b r t)")).then_inc(q_stored[t], 16)

            def after(n):
                if n == -1:
                    store_queries(0)
                if n == 0:
                    for t in range(1, TILES):
                        store_queries(t)
                    for t in range(1, TILES):
                        sp.wait_ge(q_stored[t], 16 * SLOTS)

            def load_weights(n):
                if n == B - 3:
                    for i, w in enumerate((swk_d, swv_d)):
                        sp.dma_start(swkv[:, i], w.rearrange("(c p) n -> p c n", p=P)).then_inc(swkv_loaded, 16)
                    sp.wait_ge(ctx_transposed, C * (B - 1))
                    for g in range(G):
                        sp.dma_start(wo[HD * g:HD * g + HD],
                                     xwo_d[R * HD * g:R * HD * (g + 1)].rearrange("(r d) n -> d r n", r=R)).then_inc(weights_loaded, 16)
                if n == B - 2:
                    sp.wait_ge(ctx_transposed, C * B)
                    sp.dma_start(swq, swq_d.rearrange("(c p) n -> p c n", p=P)).then_inc(swq_loaded, 16)
                    for g in range(G):
                        sp.dma_start(swo[HD * g:HD * g + HD],
                                     swo_d[R * HD * g:R * HD * (g + 1)].rearrange("(r d) n -> d r n", r=R)).then_inc(tail_weights_loaded, 16)

            slots(sp, slot, 1, after)
            for t in range(TILES):
                sp.wait_ge(out_ready, t + 1)
                sp.dma_start(of[t], xn[:, t]).then_inc(out_stored, 16)
            sp.wait_ge(out_stored, 16 * TILES)

        @block.gpsimd
        def _(pool):
            nc.gpsimd.memset(vaug[:, :, :, :, HD:VW], 1.0).then_inc(ones_ready, 1)

            nc.gpsimd.memset(zeros[:], 0.0).then_inc(zeros_ready, 1)
            pool.wait_ge(zeros_ready, 1)

            def key_parts(m, trip):
                wait(pool, k_res, 1, m, 1, trip)
                wait_ring(pool, k_stored, m - 2, trip, SLOTS)
                nc.gpsimd.tensor_tensor(kparts[:, m % 2, 1], kres[:], zeros[:], ALU.add).then_inc(k_mid, 1)
                wait(pool, k_mid, 1, m, 1, trip)
                nc.gpsimd.tensor_tensor(kparts[:, m % 2, 2], kres[:], kparts[:, m % 2, 1], ALU.subtract).then_inc(k_low, 1)

            def max_parts(m, half, trip):
                nm = negmax[:, m % 2, HALF * half:HALF * half + HALF]
                wait(pool, max_ready, G, m, HALF * (half + 1), trip)
                wait(pool, m_transposed, 2, m - 1, half + 1, trip)
                nc.gpsimd.tensor_tensor(mparts[:, half, 0], nm, zeros[:, 0:HALF], ALU.add).then_inc(mpart_high, 1)
                wait(pool, mpart_high, 2, m, half + 1, trip)
                nc.gpsimd.tensor_tensor(maxres[:, half], nm, mparts[:, half, 0], ALU.subtract).then_inc(mpart_res, 1)
                wait(pool, mpart_res, 2, m, half + 1, trip)
                nc.gpsimd.tensor_tensor(mparts[:, half, 1], maxres[:, half], zeros[:, 0:HALF], ALU.add).then_inc(mpart_mid, 1)
                wait(pool, mpart_mid, 2, m, half + 1, trip)
                nc.gpsimd.tensor_tensor(mparts[:, half, 2], maxres[:, half], mparts[:, half, 1], ALU.subtract).then_inc(mpart_ready, 1)

            def slot(n, trip):
                if live(n - 1, trip):
                    max_parts(n - 1, 1, trip)
                if splits_keys(n, 0, trip):
                    key_parts(n + 1, trip)
                if live(n, trip):
                    max_parts(n, 0, trip)
                for g in range(G):
                    early(n, g, steps)

            def queries(t):
                pool.wait_ge(sq_turned, t + 1)
                nc.gpsimd.tensor_tensor(q_rot[:, t], q_rot[:, t], rotq_b[:, t % 2], ALU.add).then_inc(q_rot_ready, 1)

            def keys_values(t):
                if t == 0:
                    pool.wait_ge(k_low, B)
                    nc.gpsimd.tensor_copy(spread, ident[:].rearrange("p (b k) -> p b k", b=BPT).unsqueeze(2).to_broadcast([P, BPT, HALF, S])
                                          ).then_inc(spread_ready, 1)
                    pool.wait_ge(consts_loaded, 80)
                pool.wait_ge(sk_turned, t + 1)
                nc.gpsimd.tensor_tensor(k_rot[:, t], k_rot[:, t], rotk_b[:, t], ALU.add).then_inc(k_rot_ready, 1)

            def heads_to_columns(t):
                pool.wait_ge(k2T_ready, t + 1)
                nc.gpsimd.tensor_tensor(kbd[:, t], k2T[:, t].rearrange("p (b k) -> p b k", b=BPT).unsqueeze(2).to_broadcast([P, BPT, G, S]),
                                        group_mask[:].unsqueeze(1).unsqueeze(3).to_broadcast([P, BPT, G, S]), ALU.mult).then_inc(kbd_ready, 1)

            def probabilities(t):
                pool.wait_ge(rsum_ready, t + 1)
                nc.gpsimd.tensor_tensor(p2[:, t], p2[:, t], ssum[:, t].unsqueeze(3).to_broadcast([P, BPT, G, S]), ALU.mult).then_inc(p2_scaled, 1)

            def transpose2(t):
                pool.wait_ge(xn_ready[1], t + 1)
                nc.gpsimd.tensor_tensor(xs[:, t], xs[:, t], bias[:], ALU.add).then_inc(x2b_ready, 1)

            nothing = lambda t: None
            steps = {step: nothing for step, _ in STEPS}
            steps.update(queries=queries, keys_values=keys_values, heads_to_columns=heads_to_columns,
                         probabilities=probabilities, transpose2=transpose2)

            def after(n):
                if n == -1:
                    wide = wnat.rearrange("p (n k) -> p n k", k=GS)
                    pool.wait_ge(packed_loaded, 32)
                    nc.gpsimd.tensor_scalar(wnorm[:, 1], wnorm[:, 0], 2.0, None, ALU.mult).then_inc(w_scaled, 1)
                    pool.wait_ge(w_scaled, 1)
                    pool.wait_ge(unpacked, 1)
                    nc.gpsimd.tensor_tensor(wide, wide, wnorm[:, 1].unsqueeze(2).to_broadcast([P, NGRP, GS]), ALU.mult).then_inc(w_step, 1)
                    pool.wait_ge(w_step, 1)
                    nc.gpsimd.tensor_tensor(wide, wide, wnorm[:, 0].unsqueeze(2).to_broadcast([P, NGRP, GS]), ALU.subtract).then_inc(w_ready, 1)
                    key_parts(1, 0)

            slots(pool, slot, 2, after)

            late(steps)

        @block.scalar
        def _(act):
            act.dma_start(ident[:], ident_d).then_inc(ident_loaded, 16)
            act.wait_ge(wkv_loaded, 32)
            nc.scalar.activation(wkv_h[:, 0].rearrange("p c (d g) -> p c d g", g=G),
                                 wkv_raw[:, 0].rearrange("p c (g d) -> p c d g", g=G), ACT.Copy).then_inc(wkv_high, 1)
            nc.scalar.activation(wkv_h[:, 1], wkv_raw[:, 1], ACT.Copy).then_inc(wkv_high, 1)
            act.wait_ge(ident_loaded, 16)
            nc.scalar.activation(ident_h[:], ident[:], ACT.Copy).then_inc(identh_ready, 1)

            def key_high(m, trip):
                wait(act, k_summed, 1, m, 1, trip)
                wait_ring(act, k_stored, m - 2, trip, SLOTS)
                nc.scalar.activation(kparts[:, m % 2, 0], b_k[:], ACT.Copy).then_inc(k_high, 1)

            def max_rows(m, half, trip):
                wait(act, m_transposed, 2, m, half + 1, trip)
                nc.scalar.activation(qstack[STACK:ROWS, m % 4, HALF * half:HALF * half + HALF],
                                     b_x[STACK:ROWS, 0:P // 2].bitcast(BF16).unsqueeze(1).to_broadcast([MROWS, HALF, P]),
                                     ACT.Copy).then_inc(mrows_ready, 1)

            def slot(n, trip):
                for g in range(G):
                    if splits_keys(n, g, trip):
                        key_high(n + 1 + g // 7, trip)
                    if g == 1 and live(n + 1, trip):
                        m = n + 1
                        wait(act, v_chunk, C, m, C, trip)
                        wait(act, v_transposed, 1, m, 0, trip)
                        nc.scalar.activation(vT[:], b_v[:], ACT.Copy).then_inc(vT_ready, 1)
                    if g % 2 == 0 and live(n + 2, trip):
                        m, c = n + 2, g // 2
                        wait(act, ctx_transposed, C, m, c + 1, trip)
                        wait(act, v_chunk, C, m - 1, c + 1, trip)
                        nc.scalar.activation(cT_h[:, c], b_t[:], ACT.Copy).then_inc(ctx_high, 1)
                        if not looped(trip):
                            head(n, g)
                    if g == 2 and live(n - 1, trip):
                        max_rows(n - 1, 1, trip)
                    if live(n - 1, trip):
                        m = n - 1
                        wait(act, st_ready, G, m, g + 1, trip)
                        wait(act, pv_ready, 2, m - 1, g // HALF + 1, trip)
                        nc.scalar.activation(pT[:, g], b_c[g % 2][:].rearrange("p (a n) -> p a n", a=KT),
                                             ACT.Exp, scale=SCALE).then_inc(exp_ready, 1)
                    if g == 2 and live(n - 2, trip):
                        m = n - 2
                        wait(act, pv_ready, 2, m, 2, trip)
                        wait(act, oraw_transposed, 1, m, 0, trip)
                        nc.scalar.activation(o_raw[:], b_d[:, 0:2 * P].rearrange("p (h n) -> p h n", h=2), ACT.Copy).then_inc(oraw_ready, 1)
                    if g == 7 and live(n, trip):
                        max_rows(n, 0, trip)
                    if (n, g) == (-1, 7):
                        for c in range(C):
                            act.wait_ge(w_transposed, c + 1)
                            nc.scalar.activation(wT_h[:, c], b_y[c % 2][:], ACT.Copy).then_inc(wT_high, 1)
                    if (n, g) in SPLIT_AT:
                        split_weights(SPLIT_AT[n, g])
                    early(n, g, steps)

            def deviation(t, norm):
                act.wait_ge(ln_var[norm], t + 1)
                nc.scalar.activation(rstd[:, t:t + 1], mv[:, t, 1:2], ACT.Sqrt).then_inc(ln_std[norm], 1)

            def transposed(t, norm):
                act.wait_ge((xn_transposed, xn2_transposed)[norm], t + 1)
                nc.scalar.activation(xnT_h[:, t], (bank_y, bank_x)[norm][t][:], ACT.Copy).then_inc((xnT_high, xnT2_high)[norm], 1)

            def split_weights(piece):
                if piece == 0:
                    act.wait_ge(v_chunk, C * B)
                if piece < 2:
                    act.wait_ge(swkv_loaded, 32)
                    nc.scalar.activation(wkv_h[:, piece], swkv[:, piece], ACT.Copy).then_inc(swkv_high, 1)
                else:
                    c = piece - 2
                    act.wait_ge(swq_loaded, 16)
                    nc.scalar.activation(swq_h[:, c], swq[:, c], ACT.Copy).then_inc(swq_high, 1)

            def heads_to_columns(t):
                act.wait_ge(q_transposed, t + 1)
                nc.scalar.activation(q2T[:, t].rearrange("p b (r t) -> p r b t", r=R),
                                     bank_x[t][:].rearrange("p (r b t) -> p r b t", r=R, b=BPT), ACT.Copy).then_inc(q2T_ready, 1)
                act.wait_ge(k_transposed, t + 1)
                nc.scalar.activation(k2T[:, t], bank_y[t][:, 0:P], ACT.Copy).then_inc(k2T_ready, 1)

            def scores(t):
                for half in range(2):
                    act.wait_ge(ss_shifted, 2 * t + half + 1)
                    pair = p2[:, t, 2 * half:2 * half + 2]
                    nc.scalar.activation(pair, pair, ACT.Exp, scale=SCALE).then_inc(p2_ready, 1)

            def transpose_probabilities(t):
                for half in range(2):
                    act.wait_ge(p_transposed, 2 * t + half + 1)
                    nc.scalar.activation(pT2[:, t, 2 * half:2 * half + 2], (bank_x, bank_y)[half][t][:].rearrange("p (b h n) -> p b h n", b=2, h=2),
                                         ACT.Copy).then_inc(pT2_ready, 1)

            def attend(t):
                act.wait_ge(so_summed, t + 1)
                nc.scalar.activation(o2T[:, t].rearrange("p r b t -> p b r t"),
                                     bank_x[t][:].rearrange("p (b r t) -> p b r t", b=BPT, r=R), ACT.Copy).then_inc(o2T_ready, 1)

            nothing = lambda t: None
            steps = {step: nothing for step, _ in STEPS}
            steps.update(residual1=lambda t: deviation(t, 0), transpose1=lambda t: transposed(t, 0), heads_to_columns=heads_to_columns,
                         scores=scores, transpose_probabilities=transpose_probabilities, attend=attend,
                         residual2=lambda t: deviation(t, 1), transpose2=lambda t: transposed(t, 1))

            def head(n, g):
                if (n, g) == (-2, 4):
                    act.wait_ge(ln1_var, 1)
                    nc.scalar.activation(rstd[:], mv[:, :, 1], ACT.Sqrt).then_inc(ln1_std, 1)
                if (n, g) == (-2, 6):
                    act.wait_ge(xwq_loaded, 16)
                    for c in (2, 3):
                        nc.scalar.activation(wq_dg[:, c].rearrange("p r (d g) -> p r d g", g=G),
                                             xwq[:, c].rearrange("p (g r d) -> p r d g", g=G, r=R), ACT.Copy).then_inc(wq_ordered, 1)
                    for t in range(TILES):
                        act.wait_ge(xh_transposed, t + 1)
                        nc.scalar.activation(xhT[:, :, P * t:P * t + P], (b_x, b_s, *b_c)[t][:].rearrange("p (c n) -> p c n", c=C),
                                             ACT.Copy).then_inc(xhT_ready, 1)
                if n == -1:
                    for r in (g // 2,):
                        act.wait_ge(q_summed, r + 1)
                        nc.scalar.activation(qparts[:, 0, :, r], b_c[r % 2][:].rearrange("p (b t) -> p b t", t=S),
                                             ACT.Copy).then_inc(q_high, 1)
                        act.wait_ge(q_res, r + 1)
                        nc.scalar.activation(qparts[:, 1, :, r], xh[:, r].rearrange("p (b t) -> p b t", t=S), ACT.Copy).then_inc(q_mid, 1)

            def after(n):
                if n == -1:
                    for i in (0, 2, 3):
                        if i >= 2:
                            act.wait_ge(unpacked, 1)
                        act.dma_start(kstack[STACK:ROWS, i].bitcast(I32), sel_d).then_inc(sel_loaded, 16)

            slots(act, slot, 2, after)

            late(steps)

        @block.vector
        def _(dve):
            nc.vector.memset(b_d[:], 0.0).then_inc(pv_zero, 1)
            dve.wait_ge(wkv_high, 2)
            nc.vector.tensor_tensor(wkv_l[:, 0].rearrange("p c (d g) -> p c d g", g=G),
                                    wkv_raw[:, 0].rearrange("p c (g d) -> p c d g", g=G),
                                    wkv_h[:, 0].rearrange("p c (d g) -> p c d g", g=G).bitcast(F32), ALU.subtract).then_inc(wkv_split, 1)
            nc.vector.tensor_tensor(wkv_l[:, 1], wkv_raw[:, 1], wkv_h[:, 1].bitcast(F32), ALU.subtract).then_inc(wkv_split, 1)

            def normalise(m, trip):
                acc = b_d[:, 2 * P:].rearrange("p (g v) -> p g v", v=TILE)
                wait(dve, oraw_transposed, 1, m, 1, trip)
                nc.vector.reciprocal(rden[:, m % 2], acc[:, :, HD]).then_inc(rden_ready, 1)
                wait(dve, rden_ready, 1, m, 1, trip)
                nc.vector.tensor_tensor(o_sb[:, m % 2], acc[:, :, 0:HD],
                                        rden[:, m % 2].unsqueeze(2).to_broadcast([P, G, HD]), ALU.mult).then_inc(o_ready, 1)

            def slot(n, trip):
                for g in range(G):
                    if live(n, trip):
                        wait(dve, s_ready, G, n, g + 1, trip)
                        if g % HALF == 0:
                            wait(dve, mpart_res, 2, n - 2, g // HALF + 1, trip)
                        nc.vector.tensor_reduce(negmax[:, n % 2, g:g + 1], b_s[:], AX, ALU.max, negate=True).then_inc(max_ready, 1)
                    if g == 6 and live(n - 2, trip):
                        m = n - 2
                        wait(dve, o_transposed, 1, m, 1, trip)
                        tile = m // BPT + trip
                        nc.vector.tensor_copy(oT[:, tile, :, S * (m % BPT):S * (m % BPT) + S],
                                              b_x[:, 0:P].rearrange("p (r t) -> p r t", r=R)).then_inc(oT_ready, 1)
                    if splits_keys(n, g, trip):
                        m = n + 1 + g // 7
                        wait(dve, k_high, 1, m, 1, trip)
                        wait(dve, k_low, 1, m - 1, 1, trip)
                        nc.vector.tensor_tensor(kres[:], b_k[:], kparts[:, m % 2, 0], ALU.subtract).then_inc(k_res, 1)
                    if g % 2 == 0 and live(n + 2, trip):
                        m, c = n + 2, g // 2
                        wait(dve, ctx_high, C, m, c + 1, trip)
                        nc.vector.tensor_tensor(cT_l[:, c], b_t[:], cT_h[:, c].bitcast(F32), ALU.subtract).then_inc(ctx_low, 1)
                        if not looped(trip):
                            head(n, g)
                    if g == 4 and live(n + 1, trip):
                        m = n + 1
                        wait(dve, v_transposed, 1, m, 1, trip)
                        nc.vector.tensor_copy(vaug[:, m % 4, :, :, 0:HD],
                                              b_x[:].rearrange("p (a g d) -> p a g d", a=KT, g=G)).then_inc(v_ready, 1)
                    if g == 3 and live(n - 2, trip):
                        normalise(n - 2, trip)
                    if (n, g) == (-1, 7):
                        for c in range(C):
                            dve.wait_ge(wT_high, c + 1)
                            nc.vector.tensor_tensor(wT_l[:, c], b_y[c % 2][:], wT_h[:, c].bitcast(F32), ALU.subtract).then_inc(wT_ready, 1)
                    if (n, g) in SPLIT_AT:
                        split_weights(SPLIT_AT[n, g])
                    early(n, g, steps)

            def unpack(piece):
                SHR, SHL, AND, OR = ALU.logical_shift_right, ALU.logical_shift_left, ALU.bitwise_and, ALU.bitwise_or
                b0, b1, b2 = (qbytes[:, :, k] for k in range(3))
                shifted = ((0, b0, 0), (1, b0, 3), (3, b1, 1), (4, b1, 4), (6, b2, 2), (7, b2, 5))
                if piece == 0:
                    dve.wait_ge(packed_loaded, 32)
                    nc.vector.tensor_copy(qbytes.rearrange("p n k -> p (n k)"),
                                          q3[:].rearrange("p t n -> p (t n)").bitcast(U8)).then_inc(unpack_step, 1)
                    dve.wait_ge(unpack_step, 1)
                    nc.vector.tensor_scalar(bits[:, 0], b0, 6, 3, SHR, AND).then_inc(unpack_step, 1)
                    nc.vector.tensor_scalar(bits[:, 1], b1, 1, 2, AND, SHL).then_inc(unpack_step, 1)
                    nc.vector.tensor_scalar(bits[:, 2], b1, 7, 1, SHR, AND).then_inc(unpack_step, 1)
                    nc.vector.tensor_scalar(bits[:, 3], b2, 3, 1, AND, SHL).then_inc(unpack_step, 1)
                if piece == 1:
                    for k, byte, shift in shifted:
                        nc.vector.tensor_scalar(qvals[:, :, k], byte, shift, 7, SHR, AND).then_inc(unpack_step, 1)
                if piece == 2:
                    dve.wait_ge(unpack_step, 11)
                    nc.vector.tensor_tensor(qvals[:, :, 2], bits[:, 0], bits[:, 1], OR).then_inc(unpack_step, 1)
                    nc.vector.tensor_tensor(qvals[:, :, 5], bits[:, 2], bits[:, 3], OR).then_inc(unpack_step, 1)
                    dve.wait_ge(unpack_step, 13)
                    nc.vector.tensor_scalar(wnat, qvals.rearrange("p n k -> p (n k)"), 1.0 / 7.0, None, ALU.mult).then_inc(unpacked, 1)

            def head(n, g):
                if (n, g) in ((-2, 0), (-2, 2)):
                    dve.wait_ge(x_loaded, 16)
                    for t in (g, g + 1):
                        nc.vector.bn_stats(st[:, t], xs[:, t]).then_inc(ln1_step, 1)
                if (n, g) == (-2, 2):
                    for t in range(TILES):
                        dve.wait_ge(ln1_step, t + 1)
                        nc.vector.bn_aggr(mv[:, t], st[:, t]).then_inc(ln1_step, 1)
                    dve.wait_ge(ln1_step, 2 * TILES)
                    nc.vector.tensor_scalar(mv[:, :, 1], mv[:, :, 1], EPS, None, ALU.add).then_inc(ln1_var, 1)
                if (n, g) == (-2, 4):
                    dve.wait_ge(ln1_std, 1)
                    nc.vector.reciprocal(rstd[:], rstd[:]).then_inc(ln1_step, 1)
                    dve.wait_ge(ln1_step, 2 * TILES + 1)
                    for t in range(TILES):
                        nc.vector.tensor_scalar(xh[:, t], xs[:, t], mv[:, t, 0:1], rstd[:, t:t + 1], ALU.subtract,
                                                ALU.mult).then_inc(xh_ready, 1)
                if (n, g) == (-2, 6):
                    dve.wait_ge(xwq_loaded, 16)
                    for c in (0, 1):
                        nc.vector.tensor_copy(wq_dg[:, c].rearrange("p r (d g) -> p r d g", g=G),
                                              xwq[:, c].rearrange("p (g r d) -> p r d g", g=G, r=R)).then_inc(wq_ordered, 1)
                if n == -1:
                    if g < 6:
                        unpack(g // 2)
                    for r in (g // 2,):
                        dve.wait_ge(q_high, r + 1)
                        nc.vector.tensor_tensor(xh[:, r].rearrange("p (b t) -> p b t", t=S),
                                                b_c[r % 2][:].rearrange("p (b t) -> p b t", t=S),
                                                qparts[:, 0, :, r], ALU.subtract).then_inc(q_res, 1)
                        dve.wait_ge(q_mid, r + 1)
                        nc.vector.tensor_tensor(qparts[:, 2, :, r], xh[:, r].rearrange("p (b t) -> p b t", t=S),
                                                qparts[:, 1, :, r], ALU.subtract).then_inc(q_low, 1)

            def residual(t, norm):
                if t == 0 and norm == 0:
                    dve.wait_ge(w_transposed, C)
                    dve.wait_ge(consts_loaded, 80)
                dve.wait_ge((wo_summed, swo_summed)[norm], t + 1)
                nc.vector.tensor_tensor(xs[:, t], (bank_x, bank_y)[norm][t][:], xs[:, t], ALU.add).then_inc((x1_ready, x2_ready)[norm], 1)
                dve.wait_ge((x1_ready, x2_ready)[norm], t + 1)
                nc.vector.bn_stats(st[:, t], xs[:, t]).then_inc(ln_stats[norm], 1)
                dve.wait_ge(ln_stats[norm], t + 1)
                nc.vector.bn_aggr(mv[:, t], st[:, t]).then_inc(ln_aggr[norm], 1)
                dve.wait_ge(ln_aggr[norm], t + 1)
                nc.vector.tensor_scalar(mv[:, t, 1:2], mv[:, t, 1:2], EPS, None, ALU.add).then_inc(ln_var[norm], 1)

            def normalise_rows(t, norm):
                dve.wait_ge(ln_std[norm], t + 1)
                nc.vector.reciprocal(rstd[:, t:t + 1], rstd[:, t:t + 1]).then_inc(ln_rstd[norm], 1)
                dve.wait_ge(ln_rstd[norm], t + 1)
                nc.vector.tensor_scalar(xn[:, t], xs[:, t], mv[:, t, 0:1], rstd[:, t:t + 1], ALU.subtract, ALU.mult).then_inc(xn_ready[norm], 1)

            def transposed(t, norm):
                dve.wait_ge((xnT_high, xnT2_high)[norm], t + 1)
                nc.vector.tensor_tensor(xnT_l[:, t], (bank_y, bank_x)[norm][t][:], xnT_h[:, t].bitcast(F32),
                                        ALU.subtract).then_inc((xnT_ready, xnT2_ready)[norm], 1)

            def split_weights(piece):
                if piece < 2:
                    dve.wait_ge(swkv_high, piece + 1)
                    nc.vector.tensor_tensor(wkv_l[:, piece], swkv[:, piece], wkv_h[:, piece].bitcast(F32), ALU.subtract).then_inc(swkv_ready, 1)
                else:
                    c = piece - 2
                    dve.wait_ge(swq_high, c + 1)
                    nc.vector.tensor_tensor(swq_l[:, c], swq[:, c], swq_h[:, c].bitcast(F32), ALU.subtract).then_inc(swq_ready, 1)

            def turn(src, a, b, shape, cs, sn, done):
                nc.vector.tensor_tensor(a, src, cs.to_broadcast(shape + [HD]), ALU.mult)
                nc.vector.tensor_tensor(b[..., 0:HD // 2], src[..., HD // 2:HD], sn[..., 0:HD // 2].to_broadcast(shape + [HD // 2]), ALU.mult)
                nc.vector.tensor_tensor(b[..., HD // 2:HD], src[..., 0:HD // 2], sn[..., HD // 2:HD].to_broadcast(shape + [HD // 2]), ALU.mult).then_inc(done, 1)

            cos = rope[:, 0].unsqueeze(1)
            sin = rope[:, 1].unsqueeze(1)

            def queries(t):
                dve.wait_ge(sq_summed, t + 1)
                count(dve, q_rot_ready, t - 1)
                a, b = (v.rearrange("p (r g d) -> p r g d", r=R, g=G) for v in (q_rot[:, t], rotq_b[:, t % 2]))
                turn(bank_x[t][:].rearrange("p (g r d) -> p r g d", g=G, r=R), a, b, [P, R, G], cos.unsqueeze(1), sin.unsqueeze(1), sq_turned)

            def keys_values(t):
                dve.wait_ge(skv_summed, t + 1)
                src, a, b = (v.rearrange("p (g d) -> p g d", g=G) for v in (bank_y[t][:, 0:KV], k_rot[:, t], rotk_b[:, t]))
                turn(src, a, b, [P, G], cos, sin, sk_turned)
                nc.vector.tensor_copy(v2[:, t], bank_y[t][:, KV:2 * KV]).then_inc(v2_ready, 1)

            def spread_values(t):
                dve.wait_ge(v_spread, t + 1)
                nc.vector.tensor_tensor(vbd[:, t].rearrange("p b (h j d) -> p (b h) j d", h=2, j=HALF),
                                        bank_x[t][:].rearrange("p (x j d) -> p x j d", j=HALF, d=HD),
                                        batch_mask[:].unsqueeze(1).unsqueeze(3).to_broadcast([P, 2 * BPT, HALF, HD]), ALU.mult).then_inc(vbd_ready, 1)

            def scores(t):
                for half in range(2):
                    k = 2 * t + half
                    src = (bank_x, bank_y)[half][t][:].rearrange("p (b g k) -> p b g k", b=2, g=G)
                    top = smax[:, t, 2 * half:2 * half + 2]
                    dve.wait_ge(ss_summed, k + 1)
                    nc.vector.tensor_reduce(top, src, AX, ALU.max).then_inc(smax_ready, 1)
                    dve.wait_ge(smax_ready, k + 1)
                    nc.vector.tensor_tensor(p2[:, t, 2 * half:2 * half + 2], src, top.unsqueeze(3).to_broadcast([P, 2, G, S]), ALU.subtract).then_inc(ss_shifted, 1)

            def probabilities(t):
                dve.wait_ge(p2_ready, 2 * t + 2)
                nc.vector.tensor_reduce(ssum[:, t], p2[:, t], AX, ALU.add).then_inc(ssum_ready, 1)
                dve.wait_ge(ssum_ready, t + 1)
                nc.vector.reciprocal(ssum[:, t], ssum[:, t]).then_inc(rsum_ready, 1)

            def feed_forward(t):
                dve.wait_ge(x2b_ready, t + 1)
                dve.wait_ge(ffn_summed, t + 1)
                nc.vector.tensor_tensor(xn[:, t], bank_y[t][:], xs[:, t], ALU.add).then_inc(out_ready, 1)

            nothing = lambda t: None
            steps = {step: nothing for step, _ in STEPS}
            steps.update(residual1=lambda t: residual(t, 0), normalise1=lambda t: normalise_rows(t, 0),
                         transpose1=lambda t: transposed(t, 0), transpose2=lambda t: transposed(t, 1), queries=queries,
                         keys_values=keys_values, spread_values=spread_values, scores=scores, probabilities=probabilities,
                         residual2=lambda t: residual(t, 1), normalise2=lambda t: normalise_rows(t, 1), feed_forward=feed_forward)
            slots(dve, slot, 2)
            late(steps)

        @block.tensor
        def _(pe):
            def ctx_chunk(m, c, trip):
                if c == 0:
                    wait_ring(pe, ctx_loaded, m, trip)
                wait(pe, ctx_low, C, m, c, trip)
                for a in range(KT):
                    last = nc.tensor.transpose(b_t[:, P * a:P * a + P], cx[:, m % 2, a, P * c:P * c + P], ident[:])
                last.then_inc(ctx_transposed, 1)

            def project(m, which, c, trip):
                wait(pe, ctx_low, C, m, c + 1, trip)
                if c == 0:
                    wait(pe, vT_ready if which else k_res, 1, m, 0, trip)
                out = (b_k, b_v)[which][:]
                nc.tensor.matmul(out, wkv_h[:, which, c], cT_h[:, c], start=(c == 0), stop=False)
                nc.tensor.matmul(out, wkv_l[:, which, c], cT_h[:, c], start=False, stop=False)
                last = nc.tensor.matmul(out, wkv_h[:, which, c], cT_l[:, c], start=False, stop=(c == C - 1))
                if which == 1:
                    last.then_inc(v_chunk, 1)
                elif c == C - 1:
                    last.then_inc(k_summed, 1)

            def max_rows(m, half, trip):
                wait(pe, mpart_ready, 2, m, half + 1, trip)
                nc.tensor.transpose(b_x[STACK:ROWS, 0:P // 2].bitcast(BF16),
                                    mparts[:, half].rearrange("p k j -> p (k j)"), ident_h[:]).then_inc(m_transposed, 1)

            def times_v(m, half, trip):
                wait(pe, exp_ready, G, m, HALF * (half + 1), trip)
                if half == 0:
                    wait(pe, v_ready, 1, m, 1, trip)
                    wait(pe, o_ready, 1, m, 0, trip)
                    if not looped(trip) and m == 0:
                        pe.wait_ge(pv_zero, 1)
                for a in range(KT):
                    for j in range(HALF):
                        g = HALF * half + j
                        last = nc.tensor.matmul(b_d[TILE * j:TILE * j + VW, P * half:P * half + P], vaug[:, m % 4, a, g],
                                                pT[:, g, a], start=(a == 0), stop=(a == KT - 1))
                last.then_inc(pv_ready, 1)

            def slot(n, trip):
                for g in range(G):
                    if live(n, trip):
                        if g == 0:
                            wait_ring(pe, kstack_loaded, n, trip)
                            wait_ring(pe, qstack_loaded, n, trip)
                        wait(pe, max_ready, G, n, g, trip)
                        nc.tensor.matmul(b_s[:], qstack[0:STACK, n % 4, g], kstack[0:STACK, n % 4, g],
                                         start=True, stop=True).then_inc(s_ready, 1)
                    if g == 0 and live(n + 2, trip):
                        ctx_chunk(n + 2, 0, trip)
                    if live(n - 1, trip):
                        m = n - 1
                        wait(pe, exp_ready, G, m, g - 1, trip)
                        if not looped(trip) and (m, g) == (0, 0):
                            pe.wait_ge(q_res, R)
                        if g % HALF == 0:
                            wait(pe, mrows_ready, 2, m, g // HALF + 1, trip)
                        for a in range(KT):
                            last = nc.tensor.matmul(b_c[g % 2][:, P * a:P * a + P], kstack[0:ROWS, m % 4, g, P * a:P * a + P],
                                                    qstack[0:ROWS, m % 4, g], start=True, stop=True)
                        last.then_inc(st_ready, 1)
                    if g == 1 and live(n - 2, trip):
                        times_v(n - 2, 1, trip)
                    if g == 6 and live(n - 1, trip):
                        times_v(n - 1, 0, trip)
                    if g == 2 and live(n - 1, trip):
                        wait(pe, mrows_ready, 2, n - 1, 1, trip)
                        max_rows(n - 1, 1, trip)
                    if g == 3 and live(n + 1, trip):
                        m = n + 1
                        wait(pe, vT_ready, 1, m, 1, trip)
                        if live(n - 1, trip):
                            wait(pe, mrows_ready, 2, n - 1, 2, trip)
                        for a in range(KT):
                            last = nc.tensor.transpose(b_x[:, P * a:P * a + P], vT[:, P * a:P * a + P], ident[:])
                        last.then_inc(v_transposed, 1)
                    if g == 3 and live(n - 2, trip):
                        m = n - 2
                        wait(pe, oraw_ready, 1, m, 1, trip)
                        for half in range(2):
                            last = nc.tensor.transpose(b_d[:, P * (2 + half):P * (3 + half)], o_raw[:, half], ident[:])
                        last.then_inc(oraw_transposed, 1)
                    if not looped(trip) and n == -2 and g == 1:
                        pe.wait_ge(wkv_split, 2)
                    if g % 2 and live(n + 2, trip) and n != -1:
                        if g < 7:
                            ctx_chunk(n + 2, g // 2 + 1, trip)
                        project(n + 2, 0, g // 2, trip)
                    if g == 5 and live(n - 2, trip):
                        m = n - 2
                        if live(n + 1, trip):
                            wait(pe, v_ready, 1, n + 1, 1, trip)
                        elif live(n - 1, trip):
                            wait(pe, mrows_ready, 2, n - 1, 2, trip)
                        wait(pe, o_ready, 1, m, 1, trip)
                        nc.tensor.transpose(b_x[:, 0:P], o_sb[:, m % 2].rearrange("p g d -> p (g d)"), ident[:]).then_inc(o_transposed, 1)
                    if g == 6 and live(n, trip):
                        if live(n + 1, trip):
                            wait(pe, v_ready, 1, n + 1, 1, trip)
                        if live(n - 2, trip):
                            wait(pe, oT_ready, 1, n - 2, 1, trip)
                        if not looped(trip) and n == 0:
                            pe.wait_ge(identh_ready, 1)
                            pe.wait_ge(sel_loaded, 64)
                        max_rows(n, 0, trip)
                    if g == 0 and live(n + 1, trip):
                        project(n + 1, 1, C - 1, trip)
                    if g in (2, 4, 6) and live(n + 2, trip) and n != -1:
                        project(n + 2, 1, g // 2 - 1, trip)
                    if not looped(trip):
                        head(n, g)
                    early(n, g, steps)

            def rows_by(lhsT, weight, chunks, out, done):
                for c in range(chunks):
                    last = nc.tensor.matmul(out, lhsT(c), weight(c), start=(c == 0), stop=(c == chunks - 1))
                last.then_inc(done, 1)

            def three_passes(x_h, x_l, w_h, w_l, out, done, chunks=range(C)):
                for c in chunks:
                    for i, (x, w) in enumerate(((x_h, w_h), (x_h, w_l), (x_l, w_h))):
                        last = nc.tensor.matmul(out, x[:, P * c:P * c + P], w(c), start=(c == 0 and i == 0), stop=(c == C - 1 and i == 2))
                if c == C - 1:
                    last.then_inc(done, 1)

            def residual1(t, r):
                pe.wait_ge(oT_ready, BPT * (t + 1))
                if t == 0 and r == 0:
                    pe.wait_ge(weights_loaded, 16 * G)
                    pe.wait_ge(tail_weights_loaded, 16 * G)
                for semaphore, value in ((wT_ready, C), (wT_ready, C), (exp_ready, G * B))[t:t + 1]:
                    pe.wait_ge(semaphore, value)
                last = nc.tensor.matmul(bank_x[t][:], oT[:, t, r], wo[:, r], start=(r == 0), stop=(r == R - 1))
                if r == R - 1:
                    last.then_inc(wo_summed, 1)

            def transpose_rows(t, norm):
                pe.wait_ge(xn_ready[norm], t + 1)
                for semaphore, value in ((vT_ready, B), (max_ready, G * B), (exp_ready, G * B))[t:t + 1] if norm == 0 else ():
                    pe.wait_ge(semaphore, value)
                for c in range(C):
                    last = nc.tensor.transpose((bank_y, bank_x)[norm][t][:, P * c:P * c + P], xn[:, t, P * c:P * c + P], ident[:])
                last.then_inc((xn_transposed, xn2_transposed)[norm], 1)

            def queries(t, c):
                pe.wait_ge(xnT_ready, t + 1)
                pe.wait_ge(swq_ready, C)
                three_passes(xnT_h[:, t], xnT_l[:, t], lambda c: swq_h[:, c], lambda c: swq_l[:, c], bank_x[t][:], sq_summed, (c,))

            def keys_values(t, c):
                pe.wait_ge(xnT_ready, t + 1)
                pe.wait_ge(swkv_ready, 2)
                three_passes(xnT_h[:, t], xnT_l[:, t], lambda c: wkv_h[:, :, c], lambda c: wkv_l[:, :, c],
                             bank_y[t][:, 0:2 * KV].rearrange("p (i n) -> p i n", i=2), skv_summed, (c,))

            def heads_to_columns(t):
                pe.wait_ge(q_rot_ready, t + 1)
                for r in range(R):
                    last = nc.tensor.transpose(bank_x[t][:, P * r:P * r + P], q_rot[:, t, P * r:P * r + P], ident[:])
                last.then_inc(q_transposed, 1)
                pe.wait_ge(k_rot_ready, t + 1)
                pe.wait_ge(v2_ready, t + 1)
                nc.tensor.transpose(bank_y[t][:, 0:P], k_rot[:, t], ident[:]).then_inc(k_transposed, 1)

            def spread_values(t):
                pe.wait_ge(q2T_ready, t + 1)
                pe.wait_ge(spread_ready, 1)
                for b in range(BPT):
                    last = nc.tensor.matmul(bank_x[t][:, P * b:P * b + P], spread[:, b].rearrange("p j k -> p (j k)"), v2[:, t],
                                            start=True, stop=True)
                last.then_inc(v_spread, 1)

            def scores(t):
                pe.wait_ge(kbd_ready, t + 1)
                pe.wait_ge(vbd_ready, t + 1)
                for half in range(2):
                    out = (bank_x, bank_y)[half][t]
                    nc.tensor.matmul(out[:], ident_h[:], causal[:], start=True, stop=False)
                    for i in range(2):
                        last = nc.tensor.matmul(out[:, G * S * i:G * S * (i + 1)], q2T[:, t, 2 * half + i],
                                                kbd[:, t, 2 * half + i].rearrange("p g k -> p (g k)"), start=False, stop=(i == 1))
                    last.then_inc(ss_summed, 1)

            def transpose_probabilities(t):
                pe.wait_ge(p2_scaled, t + 1)
                for half in range(2):
                    for x in range(4):
                        b, h = 2 * half + x // 2, x % 2
                        last = nc.tensor.transpose((bank_x, bank_y)[half][t][:, P * x:P * x + P],
                                                   p2[:, t, b, HALF * h:HALF * h + HALF].rearrange("p g k -> p (g k)"), ident[:])
                    last.then_inc(p_transposed, 1)

            def attend(t):
                pe.wait_ge(pT2_ready, 2 * t + 2)
                for b in range(BPT):
                    for h in range(2):
                        last = nc.tensor.matmul(bank_x[t][KV // 2 * h:KV // 2 * (h + 1), P * b:P * b + P],
                                                vbd[:, t, b, KV // 2 * h:KV // 2 * (h + 1)], pT2[:, t, b, h], start=True, stop=True)
                last.then_inc(so_summed, 1)

            def residual2(t):
                pe.wait_ge(o2T_ready, t + 1)
                rows_by(lambda r: o2T[:, t, r].rearrange("p b t -> p (b t)"), lambda r: swo[:, r], R, bank_y[t][:], swo_summed)

            def feed_forward(t):
                pe.wait_ge(xnT2_ready, t + 1)
                pe.wait_ge(wT_ready, C)
                three_passes(xnT_h[:, t], xnT_l[:, t], lambda c: wT_h[:, c], lambda c: wT_l[:, c], bank_y[t][:], ffn_summed)

            nothing = lambda t: None
            steps = {step: nothing for step, _ in STEPS}
            steps["residual1", "chunks"], steps["queries", "chunks"], steps["keys_values", "chunks"] = residual1, queries, keys_values
            steps.update(transpose1=lambda t: transpose_rows(t, 0),
                         heads_to_columns=heads_to_columns, spread_values=spread_values, scores=scores,
                         transpose_probabilities=transpose_probabilities, attend=attend, residual2=residual2,
                         transpose2=lambda t: transpose_rows(t, 1), feed_forward=feed_forward)

            def head(n, g):
                if (n, g) == (-2, 7):
                    for t in range(TILES):
                        pe.wait_ge(xh_ready, t + 1)
                        for c in range(C):
                            last = nc.tensor.transpose((b_x, b_s, *b_c)[t][:, P * c:P * c + P], xh[:, t, P * c:P * c + P], ident[:])
                        last.then_inc(xh_transposed, 1)
                if n == -1 and g % 2 == 0:
                    r = g // 2
                    if r > 0:
                        ctx_chunk(1, r, 0)
                    pe.wait_ge(xhT_ready, TILES)
                    pe.wait_ge(wq_ordered, C)
                    count(pe, q_res, r - 1)
                    for c in range(C):
                        last = nc.tensor.matmul(b_c[r % 2][:], wq_dg[:, c, r], xhT[:, c], start=(c == 0), stop=(c == C - 1))
                    last.then_inc(q_summed, 1)
                if (n, g) == (-1, 7):
                    for which, chunks in ((0, C), (1, C - 1)):
                        for c in range(chunks):
                            project(1, which, c, 0)
                    pe.wait_ge(w_ready, 1)
                    pe.wait_ge(ctx_low, 2 * C)
                    for c in range(C):
                        count(pe, wT_ready, c - 1)
                        for t in range(TILES):
                            at = D * t + P * c
                            last = nc.tensor.transpose(b_y[c % 2][:, P * t:P * t + P], wnat[:, at:at + P], ident[:])
                        last.then_inc(w_transposed, 1)
                    pe.wait_ge(wT_ready, C)

            pe.wait_ge(ident_loaded, 16)
            slots(pe, slot, 2)

            late(steps)


_INS = ["x", "ctx_4096", "L0_xattn_Wq", "L0_xattn_Wk", "L0_xattn_Wv", "L0_xattn_Wo", "L0_attn_Wq", "L0_attn_Wk",
        "L0_attn_Wv", "L0_attn_Wo", "L0_ffn_weight_q3", "L0_ffn_weight_norm", "L0_ffn_bias"]


def kernel(**inputs):
    import numpy as _np
    import concourse.bacc as _bacc
    from concourse import mybir as _mybir
    from concourse.bass_utils import run_bass_kernel_spmd as _run

    nc = _bacc.Bacc("TRN2", target_bir_lowering=False, num_devices=1)
    arrays = {name: _np.ascontiguousarray(inputs[name]) for name in _INS}
    arrays["L0_ffn_weight_q3"] = arrays["L0_ffn_weight_q3"].view(_np.int32)
    arrays.update(constants())
    args = []
    feeds = {}
    for name, a in arrays.items():
        feeds[f"in_{name}_dram"] = a
        args.append(nc.dram_tensor(f"in_{name}_dram", a.shape, _mybir.dt.from_np(a.dtype), kind="ExternalInput").ap())
    out = nc.dram_tensor("out_dram", (B, S, D), F32, kind="ExternalOutput").ap()
    perceiver(nc, *args, out)
    r = _run(nc, [feeds], core_ids=[0])
    return r.results[0]["out_dram"]
```
